# Optimizing a Trainium2 kernel written in Bass

```python
import numpy as np
import jax
import jax.numpy as jnp

def _softmax(x, axis=-1):
    return jax.nn.softmax(x, axis=axis)

def _gelu(x):
    return jax.nn.gelu(x, approximate=True)

def _silu(x):
    return jax.nn.silu(x)

def _sigmoid(x):
    return jax.nn.sigmoid(x)

def _layernorm(x, axis=-1, eps=1e-05):
    m = jnp.mean(x, axis=axis, keepdims=True)
    v = jnp.var(x, axis=axis, keepdims=True)
    return (x - m) / jnp.sqrt(v + eps)

def _scatter_add(tgt, idx, src, axis=0):
    return tgt.at[idx].add(src)

def _segment_sum(src, seg, n):
    return jax.ops.segment_sum(src, seg, n)
kernel_name = 'mk_macaron_d1_jaxref_r8_df53ac'

def setup_inputs(seed: int=0):
    np.random.seed(seed)
    _w = jnp.asarray

    def _L0_attn_setup():
        import jax, jax.numpy as jnp
        import numpy as np
        B, T, D, H = (64, 64, 128, 128)
        key = jax.random.key(seed)
        k1, k2, k3 = jax.random.split(key, 3)
        scale = 0.02
        return {'x': jax.random.normal(k1, (B, T, D), dtype=jnp.float32), 'Wi': jax.random.normal(k2, (H, D), dtype=jnp.float32) * scale, 'bi': jnp.zeros((H,), dtype=jnp.float32), 'Wh': jax.random.normal(k3, (H, H), dtype=jnp.float32) * scale, 'bh': jnp.zeros((H,), dtype=jnp.float32)}
    _L0_attn_in = _L0_attn_setup()

    def _L0_ffn_setup():
        import jax, jax.numpy as jnp
        import numpy as np
        B, T, D, E = (4, 128, 128, 8)
        HD = 4 * D
        key = jax.random.key(seed)
        k1, k2, k3, k4 = jax.random.split(key, 4)
        std = 0.5 * D ** (-0.5)
        bound = 3.0 ** 0.5 * std
        x = jax.random.normal(k1, (B, T, D), dtype=jnp.float32)
        router_w = jax.random.normal(k2, (E, D), dtype=jnp.float32) * 0.02
        expert_fc = jax.random.uniform(k3, (E, D, HD), dtype=jnp.float32, minval=-bound, maxval=bound)
        expert_proj = jax.random.normal(k4, (E, D, HD), dtype=jnp.float32) * 0.02
        return {'x': x, 'router_w': router_w, 'expert_fc': expert_fc, 'expert_proj': expert_proj}
    _L0_ffn_in = _L0_ffn_setup()
    _d = {'L0_attn_x': _L0_attn_in['x'], 'L0_attn_Wi': _L0_attn_in['Wi'], 'L0_attn_bi': _L0_attn_in['bi'], 'L0_attn_Wh': _L0_attn_in['Wh'], 'L0_attn_bh': _L0_attn_in['bh'], 'L0_ffn_router_w': _L0_ffn_in['router_w'], 'L0_ffn_expert_fc': _L0_ffn_in['expert_fc'], 'L0_ffn_expert_proj': _L0_ffn_in['expert_proj']}
    _x0 = _d['L0_attn_x']
    _d['L0_attn_x'] = jax.random.normal(jax.random.fold_in(jax.random.key(seed), 1), (16, 512, 128), dtype=_x0.dtype)
    del _x0
    return _d

def reference(L0_attn_x, L0_attn_Wi, L0_attn_bi, L0_attn_Wh, L0_attn_bh, L0_ffn_router_w, L0_ffn_expert_fc, L0_ffn_expert_proj):

    def _L0_attn_ref(x, Wi, bi, Wh, bh):
        import jax, jax.numpy as jnp
        import numpy as np
        B, T, D, H = (64, 64, 128, 128)
        xi = jnp.einsum('btd,hd->bth', x, Wi) + bi

        def step(h, xt):
            h_new = jnp.tanh(xt + h @ Wh.T + bh)
            return (h_new, h_new)
        h0 = jnp.zeros((x.shape[0], Wh.shape[0]), dtype=x.dtype)
        _, hs = jax.lax.scan(step, h0, jnp.swapaxes(xi, 0, 1))
        return jnp.swapaxes(hs, 0, 1)

    def _L0_ffn_ref(x, router_w, expert_fc, expert_proj):
        import jax, jax.numpy as jnp
        import numpy as np
        B, T, D, E = (4, 128, 128, 8)
        HD = 4 * D
        logits = jnp.einsum('btd,ed->bte', x, router_w)
        probs = jax.nn.softmax(logits, axis=-1)
        expert_ids = jnp.argmax(probs, axis=-1)
        mask = jax.nn.one_hot(expert_ids, E, dtype=x.dtype)
        h = jnp.einsum('btd,edh->ebth', x, expert_fc)
        h = jnp.square(jax.nn.relu(h))
        out_e = jnp.einsum('ebth,edh->ebtd', h, expert_proj)
        output = jnp.einsum('ebtd,bte->btd', out_e, mask)
        return output
    x = L0_attn_x
    x = x + 0.5 * _L0_ffn_ref(_layernorm(x, axis=-1), L0_ffn_router_w, L0_ffn_expert_fc, L0_ffn_expert_proj)
    x = x + _L0_attn_ref(_layernorm(x, axis=-1), L0_attn_Wi, L0_attn_bi, L0_attn_Wh, L0_attn_bh)
    x = x + 0.5 * _L0_ffn_ref(_layernorm(x, axis=-1), L0_ffn_router_w, L0_ffn_expert_fc, L0_ffn_expert_proj)
    return x

_drawn_inputs = setup_inputs


def setup_inputs(seed=0):
    import zlib

    import numpy as np

    out = dict(_drawn_inputs(seed))
    spreads = {'L0_attn_bi': (0.0, 0.1), 'L0_attn_bh': (0.0, 0.1)}
    factors = {}
    for name, (base, spread) in spreads.items():
        noise = np.random.default_rng([zlib.crc32(name.encode()), seed]).standard_normal(out[name].shape)
        drawn = base * np.exp(spread * noise) if base else spread * noise
        out[name] = jnp.asarray(drawn.astype(out[name].dtype))
    for name, factor in factors.items():
        out[name] = (out[name] * factor).astype(out[name].dtype)
    return out
```

```python
from contextlib import ExitStack

import concourse.bass as bass
from concourse import mybir

F32 = mybir.dt.float32
BF16 = mybir.dt.bfloat16
I32 = mybir.dt.int32
U32 = mybir.dt.uint32
ALU = mybir.AluOpType
ACT = mybir.ActivationFunctionType
AX_X = mybir.AxisListType.X
P = 128
EPS = 1e-5


def build(nc, x, Wi, bi, Wh, bh, router_w, expert_fc, expert_proj, out):
    B, T, D = x.shape
    E, _, HD = expert_fc.shape
    HC = HD // P
    TH = P // B
    BLK = 128
    NBLK = T // BLK
    JB = BLK // TH
    NT = NBLK * JB
    ZS = 512 // B
    JMAX = 2 * JB
    TMAX = JMAX + E

    class Chunk:
        pass

    def plan(spans, first):
        chunks, g0, q0, m0 = [], first[0], first[1], first[2]
        for i, (blk, nblk) in enumerate(spans):
            c = Chunk()
            c.index, c.blk, c.nblk = first[3] + i, blk, nblk
            c.n0, c.J = blk * JB, nblk * JB
            c.S = c.J + E - 1
            c.NP = (c.S + 1) // 2
            c.g0, c.q0, c.m0 = g0, q0, m0
            c.par = c.index % 2
            g0, q0, m0 = g0 + c.S, q0 + c.NP, m0 + c.J
            chunks.append(c)
        return chunks, (g0, q0, m0, first[3] + len(spans))

    ffn1, after = plan([(0, 1), (1, 1), (2, 2)], (0, 0, 0, 0))
    ffn2, after = plan([(0, 2), (2, 1), (3, 1)], after)

    with ExitStack() as ctx:
        def sb(name, shape, dt=F32):
            return ctx.enter_context(nc.sbuf_tensor(name, shape, dt))

        def psum(name):
            return ctx.enter_context(nc.psum_tensor(name, [P, 512], F32))

        def sem(name):
            return ctx.enter_context(nc.semaphore(name))

        xs_dram = [nc.dram_tensor(f"xs_dram{i}", [TMAX * P, D], F32).ap() for i in range(2)]
        ys_dram = [nc.dram_tensor(f"ys_dram{i}", [TMAX * P, D], F32).ap() for i in range(2)]

        x_sb = sb("x_sb", [P, NT, D])
        xnf = sb("xnf", [P, JMAX, D])
        xns = sb("xns", [P, JB, D])
        back = sb("back", [P, JMAX, D])
        xnT = sb("xnT", [P, JB, P])
        hsT = sb("hsT", [P, (T + 1) * B])
        fc_sb = sb("fc_sb", [P, E * HD])
        projT = sb("projT", [P, E, HC, D])
        proj_raw = back[:, :, :].rearrange("p a b -> p (a b)")[:, 0:E * HD].rearrange("p (e h) -> p e h", e=E)
        w_raw = sb("w_raw", [P, 2, D])
        rw_raw = sb("rw_raw", [E, D])
        wT = sb("wT", [P, 2 * P + E])
        WiT, WhT, rwT = wT[:, 0:P], wT[:, P:2 * P], wT[:, 2 * P:2 * P + E]
        bias2 = sb("bias2", [P, 2])
        bias = sb("bias", [P, 1])
        ident = sb("ident", [P, P])
        before = sb("before", [P, P], BF16)
        ones = sb("ones", [P, P], BF16)
        zeros = sb("zeros", [P, 512])
        kio_i = sb("kio_i", [P, 64], I32)
        kio = sb("kio", [P, 64])
        thr = sb("thr", [P, JMAX])
        pref = sb("pref", [P, E])
        lower = sb("lower", [P, E, E])
        warm = sb("warm", [P, 1])
        stats = sb("stats", [P, JMAX, 6])
        mv = sb("mv", [P, JMAX, 2])
        rstd = sb("rstd", [P, JMAX])
        var_eps = sb("var_eps", [P, JMAX])
        newton = sb("newton", [P, JMAX])
        root_bits = sb("root_bits", [P, JMAX], I32)
        xrt = sb("xrt", [P, 2, 512])
        best = sb("best", [P, JMAX])
        eq = sb("eq", [P, JMAX, E])
        wgt = sb("wgt", [P, JMAX, E])
        oh = sb("oh", [P, JMAX, E], BF16)
        cmp = sb("cmp", [P, E, JMAX])
        ntile = sb("ntile", [P, E])
        tmp8 = sb("tmp8", [P, E, E])
        first_tile = sb("first_tile", [P, E])
        end_tile = sb("end_tile", [P, E])
        posw = sb("posw", [P, JMAX, E])
        posf = sb("posf", [P, JMAX])
        pos = sb("pos", [P, 2, JMAX], I32)
        cmp2 = sb("cmp2", [P, TMAX, E])
        exf = sb("exf", [P, TMAX])
        eoff = sb("eoff", [P, 2, TMAX], I32)
        xs_sb = sb("xs_sb", [P, 4, D])
        xT_sb = sb("xT_sb", [P, 2, P])
        r_sb = sb("r_sb", [P, 2, HD])
        s_sb = sb("s_sb", [P, 2, HC, P])
        y_sb = sb("y_sb", [P, 4, D])

        z = ctx.enter_context(nc.psum_tensor("z", [P, 2, 512], F32))
        mT = psum("mT")
        xTp, hp, rTp, yp, lg = psum("xTp"), psum("hp"), psum("rTp"), psum("yp"), psum("lg")

        s_in = sem("s_in")
        s_w = sem("s_w")
        s_fc = sem("s_fc")
        s_pr = sem("s_pr")
        s_const = sem("s_const")
        s_kc = sem("s_kc")
        s_zero = sem("s_zero")
        s_dve = sem("s_dve")
        s_tr = sem("s_tr")
        s_evac = sem("s_evac")
        s_xnf = sem("s_xnf")
        s_xns = sem("s_xns")
        s_rt = sem("s_rt")
        s_oh = sem("s_oh")
        s_rank = sem("s_rank")
        s_pos = sem("s_pos")
        s_eoff = sem("s_eoff")
        s_scat = sem("s_scat")
        s_load = sem("s_load")
        s_t0 = sem("s_t0")
        s_xt = sem("s_xt")
        s_m1 = sem("s_m1")
        s_relu = sem("s_relu")
        s_rtr = sem("s_rtr")
        s_sq = sem("s_sq")
        s_m2 = sem("s_m2")
        s_y = sem("s_y")
        s_store = sem("s_store")
        s_gath = sem("s_gath")
        s_comb = sem("s_comb")
        s_xi = sem("s_xi")
        s_z = sem("s_z")
        s_mm = sem("s_mm")
        s_h = sem("s_h")
        s_out = sem("s_out")

        block = ctx.enter_context(nc.Block())

        def tokens(dram, blk):
            return dram[:, blk * BLK:(blk + 1) * BLK, :].rearrange("b (th j) d -> th b (j d)", th=TH)

        def sb_block(blk):
            return x_sb[:, blk * JB:(blk + 1) * JB, :].rearrange("p j d -> p (j d)")

        def state(t):
            blk, r = divmod(t, BLK)
            th, j = divmod(r, JB)
            at = B + blk * BLK * B + j * P + th * B
            return hsT[:, at:at + B]

        @block.sync
        def _(sp):
            for blk in range(NBLK):
                sp.dma_start(sb_block(blk), tokens(x, blk)).then_inc(s_in, 16)
                if blk == 0:
                    sp.dma_start(w_raw[:, 0, :], Wi).then_inc(s_w, 16)
                    sp.dma_start(w_raw[:, 1, :], Wh).then_inc(s_w, 16)
                    sp.dma_start(rw_raw[:, :], router_w).then_inc(s_w, 16)
                    sp.dma_start(bias2[:, 0:1], bi.rearrange("(p a) -> p a", a=1)).then_inc(s_w, 16)
                    sp.dma_start(bias2[:, 1:2], bh.rearrange("(p a) -> p a", a=1)).then_inc(s_w, 16)
                    sp.dma_start(fc_sb[:, :].rearrange("p (e h) -> p e h", e=E),
                                 expert_fc.rearrange("e d h -> d e h")).then_inc(s_fc, 16)
                    sp.dma_start(proj_raw, expert_proj.rearrange("e d h -> d e h")).then_inc(s_pr, 16)
                    sp.wait_ge(s_const, 1)
                    for i in range(2):
                        sp.dma_start(xs_dram[i].rearrange("(p r c) d -> p r (c d)", p=P, c=4),
                                     zeros[:, :].unsqueeze(1).to_broadcast([P, TMAX // 4, 512])).then_inc(s_zero, 16)

            def load(c, q, k):
                sp.wait_ge(s_load, 16 * (c.q0 + q))
                sp.dma_start(xs_sb[:, bass.ds(k * 2, 2), :],
                             xs_dram[c.par][bass.ds(q * 2 * P, 2 * P), :].rearrange("(a p) d -> p a d", p=P)
                             ).then_inc(s_load, 16)

            def store(c, q, k, n=2):
                sp.wait_ge(s_store, 16 * (c.q0 + q))
                sp.dma_start(ys_dram[c.par][bass.ds(q * 2 * P, n * P), :].rearrange("(a p) d -> p a d", p=P),
                             y_sb[:, bass.ds(k * 2, n), :]).then_inc(s_store, 16)

            def slot_tiles(c):
                sp.wait_ge(s_scat, 16 * (c.m0 + c.J))
                if c.g0:
                    sp.wait_ge(s_t0, c.g0)
                if c.q0:
                    sp.wait_ge(s_load, 16 * c.q0)
                sp.dma_start(xs_sb[:, 0:2, :], xs_dram[c.par][0:2 * P, :].rearrange("(a p) d -> p a d", p=P)
                             ).then_inc(s_load, 16)
                load(c, 1, 1)
                with sp.Fori(0, c.NP - 2) as q:
                    sp.wait_ge(s_y, c.g0 + q * 2 + 2)
                    sp.dma_start(ys_dram[c.par][bass.ds(q * 2 * P, 2 * P), :].rearrange("(a p) d -> p a d", p=P),
                                 y_sb[:, bass.ds((q % 2) * 2, 2), :]).then_inc(s_store, 16)
                    sp.wait_ge(s_store, 16 * (c.q0 + q) + 16)
                    load(c, q + 2, q % 2)
                for q, n in ((c.NP - 2, 2), (c.NP - 1, 1)):
                    sp.wait_ge(s_y, c.g0 + min(2 * q + 2, c.S))
                    store(c, q, q % 2, n)

            for c in ffn1:
                slot_tiles(c)
            for c in ffn2:
                slot_tiles(c)
                sp.wait_ge(s_comb, c.index + 1)
                for blk in range(c.blk, c.blk + c.nblk):
                    sp.dma_start(tokens(out, blk), sb_block(blk)).then_inc(s_out, 16)
            sp.wait_ge(s_zero, 32)
            sp.wait_ge(s_store, 16 * after[1])
            sp.wait_ge(s_out, 16 * NBLK)

        @block.gpsimd
        def _(pool):
            pool.memset(zeros[:, :], 0.0).then_inc(s_const, 1)
            pool.memset(hsT[:, 0:B], 0.0).then_inc(s_const, 1)
            pool.memset(ident[:, :], 0.0).then_inc(s_const, 1)
            pool.memset(before[:, :], 1.0).then_inc(s_const, 1)
            pool.memset(ones[:, :], 1.0).then_inc(s_const, 1)
            pool.iota(kio_i[:, :], pattern=[[1, 64]], base=0, channel_multiplier=0).then_inc(s_const, 1)
            pool.wait_ge(s_const, 6)
            pool.affine_select(out=ident[:, :], in_=ident[:, :], compare_op=ALU.not_equal, fill=1.0, base=0,
                               pattern=[[-1, P]], channel_multiplier=1).then_inc(s_const, 1)
            pool.affine_select(out=before[:, :], in_=before[:, :], compare_op=ALU.is_gt, fill=0.0, base=0,
                               pattern=[[1, P]], channel_multiplier=-1).then_inc(s_const, 1)

            def scatter(c):
                pool.wait_ge(s_pos, c.index + 1)
                pool.wait_ge(s_xnf, c.m0 + c.J)
                if c.index == 0:
                    pool.wait_ge(s_zero, 32)
                if c.index >= 2:
                    pool.wait_ge(s_load, 16 * c.q0)
                for j in range(c.J):
                    pool.indirect_dma_start(
                        out=xs_dram[c.par], out_offset=bass.IndirectOffsetOnAxis(ap=pos[:, c.par, j:j + 1].bitcast(U32), axis=0),
                        in_=xnf[:, j, :], in_offset=None).then_inc(s_scat, 16)

            def gather(c):
                pool.wait_ge(s_store, 16 * (c.q0 + c.NP))
                if c.index:
                    pool.wait_ge(s_comb, c.index)
                else:
                    pool.wait_ge(s_evac, E)
                for j in range(c.J):
                    pool.indirect_dma_start(
                        out=back[:, j, :], out_offset=None,
                        in_=ys_dram[c.par][0:c.S * P, :], in_offset=bass.IndirectOffsetOnAxis(ap=pos[:, c.par, j:j + 1].bitcast(U32), axis=0)
                    ).then_inc(s_gath, 16)

            for c in ffn1 + ffn2:
                scatter(c)
                gather(c)

        @block.vector
        def _(dve):
            chain = [0]
            groups = [0]

            def link(ins):
                chain[0] += 1
                ins.then_inc(s_dve, 1)
                dve.wait_ge(s_dve, chain[0])

            def evacuate(op):
                dve.wait_ge(s_tr, groups[0] + 1)
                groups[0] += 1
                op().then_inc(s_evac, 1)

            def inverse_root(J):
                v, y, t, r = var_eps[:, 0:J], rstd[:, 0:J], newton[:, 0:J], root_bits[:, 0:J]
                link(dve.tensor_scalar(v, mv[:, 0:J, 1], EPS, None, ALU.add))
                link(dve.tensor_scalar(r, v.bitcast(I32), 1, None, ALU.arith_shift_right))
                link(dve.tensor_scalar(y.bitcast(I32), r, -1.0, float(0x5F3759DF), ALU.mult, ALU.add))
                for _ in range(4):
                    link(dve.tensor_tensor(t, y, y, ALU.mult))
                    link(dve.scalar_tensor_tensor(out=t, in0=t, scalar=-0.5, in1=v, op0=ALU.mult, op1=ALU.mult))
                    link(dve.scalar_tensor_tensor(out=y, in0=t, scalar=1.5, in1=y, op0=ALU.add, op1=ALU.mult))

            def layernorm(n0, J, dst, done):
                with dve.Fori(0, J) as j:
                    dve.bn_stats(stats[:, j, :], x_sb[:, j + n0, :]).then_inc(s_dve, 1)
                chain[0] += J
                dve.wait_ge(s_dve, chain[0])
                for j in range(J):
                    dve.bn_aggr(mv[:, j, :], stats[:, j, :]).then_inc(s_dve, 1)
                chain[0] += J
                dve.wait_ge(s_dve, chain[0])
                inverse_root(J)
                for j in range(J):
                    dve.tensor_scalar(dst[:, j, :], x_sb[:, j + n0, :], mv[:, j, 0:1], rstd[:, j:j + 1],
                                      ALU.subtract, ALU.mult).then_inc(done, 1)

            def route(c):
                J, S = c.J, c.S
                lg3 = lg[:, 0:J * E].rearrange("p (j e) -> p j e", e=E)
                rk3 = lg[:, 0:(J + 1) * E].rearrange("p (j e) -> p j e", e=E)
                for g in range(J // 4):
                    n = c.m0 // 4 + g
                    if n >= 2:
                        dve.wait_ge(s_rt, n - 1)
                    evacuate(lambda: dve.tensor_copy(xrt[:, g % 2, :], mT[:, :]))
                dve.wait_ge(s_rt, (c.m0 + J) // 4)
                link(dve.tensor_reduce(best[:, 0:J], lg3, AX_X, ALU.max))
                link(dve.tensor_tensor(eq[:, 0:J, :], lg3, best[:, 0:J].unsqueeze(2).to_broadcast([P, J, E]), ALU.is_ge))
                link(dve.tensor_tensor(wgt[:, 0:J, :], eq[:, 0:J, :], pref[:, :].unsqueeze(1).to_broadcast([P, J, E]), ALU.mult))
                link(dve.tensor_reduce(best[:, 0:J], wgt[:, 0:J, :], AX_X, ALU.max))
                dve.tensor_tensor(oh[:, 0:J, :], wgt[:, 0:J, :], best[:, 0:J].unsqueeze(2).to_broadcast([P, J, E]),
                                  ALU.is_equal).then_inc(s_oh, 1)
                dve.wait_ge(s_oh, c.index + 1)
                dve.wait_ge(s_rank, c.index + 1)
                link(dve.tensor_tensor(cmp[:, :, 0:J], rk3[:, J, :].unsqueeze(2).to_broadcast([P, E, J]),
                                       thr[:, 0:J].unsqueeze(1).to_broadcast([P, E, J]), ALU.is_gt))
                link(dve.tensor_reduce(ntile[:, :], cmp[:, :, 0:J], AX_X, ALU.add))
                link(dve.tensor_tensor(tmp8[:, :, :], lower[:, :, :], ntile[:, :].unsqueeze(1).to_broadcast([P, E, E]), ALU.mult))
                link(dve.tensor_reduce(first_tile[:, :], tmp8[:, :, :], AX_X, ALU.add))
                link(dve.tensor_tensor(end_tile[:, :], first_tile[:, :], ntile[:, :], ALU.add))
                link(dve.scalar_tensor_tensor(out=posw[:, 0:J, :], in0=first_tile[:, :].unsqueeze(1).to_broadcast([P, J, E]),
                                              scalar=float(P), in1=rk3[:, 0:J, :], op0=ALU.mult, op1=ALU.add))
                link(dve.tensor_tensor(posw[:, 0:J, :], posw[:, 0:J, :], oh[:, 0:J, :], ALU.mult))
                link(dve.tensor_reduce(posf[:, 0:J], posw[:, 0:J, :], AX_X, ALU.add))
                dve.tensor_scalar(pos[:, c.par, 0:J], posf[:, 0:J], float(S * P - 1), None, ALU.min).then_inc(s_pos, 1)
                link(dve.tensor_tensor(cmp2[:, 0:S, :], kio[:, 0:S].unsqueeze(2).to_broadcast([P, S, E]),
                                       end_tile[:, :].unsqueeze(1).to_broadcast([P, S, E]), ALU.is_ge))
                link(dve.tensor_reduce(exf[:, 0:S], cmp2[:, 0:S, :], AX_X, ALU.add))
                dve.tensor_scalar(eoff[:, c.par, 0:S], exf[:, 0:S], float(E - 1), float(HD), ALU.min, ALU.mult
                                  ).then_inc(s_eoff, 1)

            def copy_xT(c, k, u):
                dve.wait_ge(s_t0, c.g0 + k + 1)
                if not isinstance(k, int) or c.g0 + k >= 2:
                    dve.wait_ge(s_m1, c.g0 + k - 1)
                dve.tensor_copy(xT_sb[:, u % 2, :], xTp[:, 0:P]).then_inc(s_xt, 1)

            def relu(c, k, u):
                dve.wait_ge(s_m1, c.g0 + k + 1)
                if not isinstance(k, int) or c.g0 + k >= 2:
                    dve.wait_ge(s_rtr, c.g0 + k - 1)
                dve.tensor_scalar(r_sb[:, u % 2, :], hp[:, :], 0.0, None, ALU.max).then_inc(s_relu, 1)

            def halve(c, k, u):
                dve.wait_ge(s_m2, c.g0 + k + 1)
                if not isinstance(k, int) or c.q0 + k // 2 >= 2:
                    dve.wait_ge(s_store, 16 * (c.q0 + k // 2 - 1))
                dve.tensor_scalar(y_sb[:, u % 4, :], yp[:, 0:D], 0.5, None, ALU.mult).then_inc(s_y, 1)

            def slot_tiles(c):
                copy_xT(c, 0, 0)
                relu(c, 0, 0)
                copy_xT(c, 1, 1)
                relu(c, 1, 1)
                copy_xT(c, 2, 2)
                halve(c, 0, 0)
                with dve.Fori(0, (c.S - 3) // 4) as i:
                    for u in range(4):
                        relu(c, i * 4 + (2 + u), 2 + u)
                        copy_xT(c, i * 4 + (3 + u), 3 + u)
                        dve.wait_ge(s_m2, c.g0 + i * 4 + (2 + u))
                        if u % 2:
                            dve.wait_ge(s_store, 16 * (c.q0 - 1 + (1 + u) // 2) + i * 32)
                        dve.tensor_scalar(y_sb[:, (1 + u) % 4, :], yp[:, 0:D], 0.5, None, ALU.mult).then_inc(s_y, 1)
                k = c.S - 1
                relu(c, k, k)
                halve(c, k - 1, k - 1)
                halve(c, k, k)

            def combine(c):
                dve.wait_ge(s_gath, 16 * (c.m0 + c.J))
                v = x_sb[:, c.n0:c.n0 + c.J, :].rearrange("p j d -> p (j d)")
                dve.tensor_tensor(v, v, back[:, 0:c.J, :].rearrange("p j d -> p (j d)"), ALU.add).then_inc(s_comb, 1)
                dve.wait_ge(s_comb, c.index + 1)

            dve.wait_ge(s_const, 8)
            link(dve.tensor_copy(kio[:, :], kio_i[:, :]))
            dve.tensor_scalar(thr[:, :], kio[:, 0:JMAX], float(P), None, ALU.mult).then_inc(s_kc, 1)
            dve.tensor_scalar(pref[:, :], kio[:, 0:E], -1.0, float(E), ALU.mult, ALU.add).then_inc(s_kc, 1)
            dve.tensor_tensor(lower[:, :, :], kio[:, 0:E].unsqueeze(1).to_broadcast([P, E, E]),
                              kio[:, 0:E].unsqueeze(2).to_broadcast([P, E, E]), ALU.is_lt).then_inc(s_kc, 1)
            for e in range(E):
                evacuate(lambda: dve.tensor_copy(projT[:, e, :, :].rearrange("p c d -> p (c d)"), mT[:, :]))
            evacuate(lambda: dve.tensor_copy(wT[:, :], mT[:, 0:2 * P + E]))
            dve.wait_ge(s_w, 80)
            dve.tensor_tensor(bias[:, :], bias2[:, 0:1], bias2[:, 1:2], ALU.add).then_inc(s_kc, 1)
            dve.wait_ge(s_kc, 4)
            dve.wait_ge(s_in, 16 * NBLK)

            for c in ffn1:
                if c.index:
                    dve.wait_ge(s_scat, 16 * c.m0)
                layernorm(c.n0, c.J, xnf, s_xnf)
                route(c)
                slot_tiles(c)
                combine(c)

            for blk in range(NBLK):
                layernorm(blk * JB, JB, xns, s_xns)
                for g in range(JB // 4):
                    evacuate(lambda: dve.tensor_copy(xnT[:, 4 * g:4 * g + 4, :].rearrange("p j t -> p (j t)"), mT[:, :]))
                NZ = BLK // ZS
                for zc in range(blk * NZ, (blk + 1) * NZ):
                    dve.wait_ge(s_xi, zc + 1)
                    zb = z[:, zc % 2, :]
                    dve.tensor_scalar(zb, zb, bias[:, 0:1], None, ALU.add).then_inc(s_z, 1)

            for c in ffn2:
                for g in range(c.J // 4):
                    v = x_sb[:, c.n0 + 4 * g:c.n0 + 4 * g + 4, :].rearrange("p j d -> p (j d)")
                    evacuate(lambda: dve.tensor_tensor(v, v, mT[:, :], ALU.add))
                dve.wait_ge(s_evac, groups[0])
                dve.wait_ge(s_scat, 16 * c.m0)
                layernorm(c.n0, c.J, xnf, s_xnf)
                route(c)
                slot_tiles(c)
                combine(c)

        @block.scalar
        def _(act):
            act.wait_ge(s_const, 1)
            act.activation(warm[:, :], zeros[:, 0:1], ACT.Tanh)

            def square(c, k, u):
                act.wait_ge(s_rtr, c.g0 + k + 1)
                if not isinstance(k, int) or c.g0 + k >= 2:
                    act.wait_ge(s_m2, c.g0 + k - 1)
                act.activation(s_sb[:, u, :, :].rearrange("p c t -> p (c t)"), rTp[:, :], ACT.Square).then_inc(s_sq, 1)

            def slot_tiles(c):
                square(c, 0, 0)
                square(c, 1, 1)
                square(c, 2, 0)
                with act.Fori(0, (c.S - 3) // 2) as i:
                    square(c, i * 2 + 3, 1)
                    square(c, i * 2 + 4, 0)

            for c in ffn1:
                slot_tiles(c)
            with act.Fori(0, T // ZS) as zc:
                for s in range(ZS):
                    act.wait_ge(s_mm, zc * ZS + (s + 1))
                    at = (zc // (BLK // ZS)) * (BLK * B) + (zc % (BLK // ZS)) * (ZS // JB * B)
                    act.activation(hsT[:, bass.ds(at + (B + (s // JB) * B + (s % JB) * P), B)],
                                   z[:, zc % 2, s * B:(s + 1) * B], ACT.Tanh).then_inc(s_h, 1)
            for c in ffn2:
                slot_tiles(c)

        @block.tensor
        def _(pe):
            groups = [0]

            def transpose4(ins):
                if groups[0]:
                    pe.wait_ge(s_evac, groups[0])
                groups[0] += 1
                at = 0
                for a in ins:
                    rows = a.shape[0]
                    last = pe.transpose(mT[:, at:at + rows], a, ident[0:rows, 0:rows])
                    at += rows
                last.then_inc(s_tr, 1)

            def route(c):
                def products(g):
                    n = c.m0 // 4 + g
                    pe.wait_ge(s_evac, groups_at[g])
                    for q in range(4):
                        j = 4 * g + q
                        mm = pe.matmul(lg[:, j * E:(j + 1) * E], xrt[:, g % 2, q * P:(q + 1) * P], rwT, start=True, stop=True)
                    mm.then_inc(s_rt, 1)
                groups_at = {}
                if c.index:
                    pe.wait_ge(s_eoff, c.index)
                for g in range(c.J // 4):
                    pe.wait_ge(s_xnf, c.m0 + 4 * g + 4)
                    transpose4([xnf[:, 4 * g + q, :] for q in range(4)])
                    groups_at[g] = groups[0]
                    if g:
                        products(g - 1)
                products(c.J // 4 - 1)
                pe.wait_ge(s_oh, c.index + 1)
                n = c.J * E
                ohc = oh[:, 0:c.J, :].rearrange("p j e -> p (j e)")
                pe.matmul(lg[:, 0:n], before[:, :], ohc, start=True, stop=False, skip_group_check=True)
                for s in range(1, c.J + 1):
                    mm = pe.matmul(lg[:, s * E:n + E], ones[:, :], ohc[:, 0:n + E - s * E], start=False,
                                   stop=(s == c.J), skip_group_check=True)
                mm.then_inc(s_rank, 1)

            def offset(c, k):
                return pe.value_load(eoff[0:1, c.par, bass.ds(k, 1)] if not isinstance(k, int) else eoff[0:1, c.par, k:k + 1],
                                     min_val=0, max_val=(E - 1) * HD)

            def turn_x(c, k, u):
                pe.wait_ge(s_load, 16 * (c.q0 + k // 2 + 1) if isinstance(k, int) else 16 * (c.q0 + 1 + u // 2) + (k - u) * 8)
                if not isinstance(k, int) or c.g0 + k:
                    pe.wait_ge(s_xt, c.g0 + k)
                pe.transpose(xTp[:, 0:P], xs_sb[:, u % 4, :], ident[:, :]).then_inc(s_t0, 1)

            def product1(c, k, u, off):
                pe.wait_ge(s_xt, c.g0 + k + 1)
                if not isinstance(k, int) or c.g0 + k:
                    pe.wait_ge(s_relu, c.g0 + k)
                pe.matmul(hp[:, :], xT_sb[:, u % 2, :], fc_sb[:, bass.ds(off, HD)], start=True, stop=True).then_inc(s_m1, 1)

            def turn_r(c, k, u):
                pe.wait_ge(s_relu, c.g0 + k + 1)
                if not isinstance(k, int) or c.g0 + k:
                    pe.wait_ge(s_sq, c.g0 + k)
                for h in range(HC):
                    mm = pe.transpose(rTp[:, h * P:(h + 1) * P], r_sb[:, u % 2, h * P:(h + 1) * P], ident[:, :])
                mm.then_inc(s_rtr, 1)

            def product2(c, k, u, off):
                pe.wait_ge(s_sq, c.g0 + k + 1)
                if not isinstance(k, int) or c.g0 + k:
                    pe.wait_ge(s_y, c.g0 + k)
                pf = projT[:, :, :, :].rearrange("p e c d -> p (e c d)")
                for h in range(HC):
                    mm = pe.matmul(yp[:, 0:D], s_sb[:, u % 2, h, :], pf[:, bass.ds(off + h * D, D)],
                                   start=(h == 0), stop=(h == HC - 1))
                mm.then_inc(s_m2, 1)

            def slot_tiles(c):
                pe.wait_ge(s_eoff, c.index + 1)
                off0 = offset(c, 0)
                off1 = offset(c, 1)
                turn_x(c, 0, 0)
                product1(c, 0, 0, off0)
                turn_x(c, 1, 1)
                turn_r(c, 0, 0)
                product1(c, 1, 1, off1)
                turn_x(c, 2, 2)
                product2(c, 0, 0, off0)
                turn_r(c, 1, 1)
                with pe.Fori(0, (c.S - 3) // 4) as i:
                    offs = [offset(c, i * 4 + (1 + u)) for u in range(5)]
                    for u in range(4):
                        k = i * 4 + (2 + u)
                        product1(c, k, 2 + u, offs[u + 1])
                        pe.wait_ge(s_load, 16 * (c.q0 + 1 + (3 + u) // 2) + i * 32)
                        pe.wait_ge(s_xt, c.g0 + i * 4 + (3 + u))
                        pe.transpose(xTp[:, 0:P], xs_sb[:, (3 + u) % 4, :], ident[:, :]).then_inc(s_t0, 1)
                        product2(c, i * 4 + (1 + u), 1 + u, offs[u])
                        turn_r(c, k, 2 + u)
                k = c.S - 1
                offa, offb = offset(c, k - 1), offset(c, k)
                product1(c, k, k, offb)
                product2(c, k - 1, k - 1, offa)
                turn_r(c, k, k)
                product2(c, k, k, offb)

            pe.wait_ge(s_const, 8)
            pe.wait_ge(s_pr, 16)
            for e in range(E):
                transpose4([proj_raw[:, e, h * P:(h + 1) * P] for h in range(HC)])
            pe.wait_ge(s_w, 80)
            transpose4([w_raw[:, 0, :], w_raw[:, 1, :], rw_raw[:, :]])
            pe.wait_ge(s_evac, groups[0])
            pe.wait_ge(s_fc, 16)

            for c in ffn1:
                route(c)
                slot_tiles(c)

            def inputs(zc, s):
                th = s // JB
                pe.matmul(z[:, zc % 2, :], WiT, xnT[:, :, th * B:th * B + ZS // JB * B].rearrange("p j (th b) -> p th j b", b=B),
                          start=True, stop=False,
                          skip_group_check=True).then_inc(s_xi, 1)

            for blk in range(NBLK):
                for g in range(JB // 4):
                    pe.wait_ge(s_xns, blk * JB + 4 * g + 4)
                    transpose4([xns[:, 4 * g + q, :] for q in range(4)])
                pe.wait_ge(s_evac, groups[0])
                NZ = BLK // ZS
                if blk:
                    pe.wait_ge(s_h, (blk * NZ - 1) * ZS)
                inputs(blk * NZ, 0)
                for w in range(NZ):
                    zc = blk * NZ + w
                    if w + 1 < NZ:
                        if zc:
                            pe.wait_ge(s_h, zc * ZS)
                        inputs(zc + 1, (w + 1) * ZS)
                    pe.wait_ge(s_z, zc + 1)
                    for s in range(ZS):
                        t = zc * ZS + s
                        if t:
                            pe.wait_ge(s_h, t)
                        pe.matmul(z[:, zc % 2, s * B:(s + 1) * B], WhT, state(t - 1), start=False, stop=True,
                                  skip_group_check=True).then_inc(s_mm, 1)

            for c in ffn2:
                for g in range(c.J // 4):
                    pe.wait_ge(s_h, T)
                    ins = []
                    for q in range(4):
                        blk, j = divmod(4 * g + q, JB)
                        at = B + (c.blk + blk) * BLK * B + j * P
                        ins.append(hsT[:, at:at + P])
                    transpose4(ins)
                route(c)
                slot_tiles(c)


_INS = ['L0_attn_x', 'L0_attn_Wi', 'L0_attn_bi', 'L0_attn_Wh', 'L0_attn_bh', 'L0_ffn_router_w', 'L0_ffn_expert_fc',
        'L0_ffn_expert_proj']
_OUTS = [((16, 512, 128), 'float32')]


def kernel(**inputs):
    import numpy as _np
    import concourse.bacc as _bacc
    from concourse import mybir as _mybir
    from concourse.bass_utils import run_bass_kernel_spmd as _run

    nc = _bacc.Bacc("TRN2", target_bir_lowering=False, num_devices=1)
    arrays, args = {}, []
    for name in _INS:
        a = _np.ascontiguousarray(inputs[name])
        arrays[f"in_{name}_dram"] = a
        args.append(nc.dram_tensor(f"in_{name}_dram", a.shape, _mybir.dt.from_np(a.dtype), kind="ExternalInput").ap())
    for i, (shape, dtype) in enumerate(_OUTS):
        dt = _mybir.dt.from_np(_np.dtype(dtype))
        args.append(nc.dram_tensor(f"out_{i}_dram", shape, dt, kind="ExternalOutput").ap())
    build(nc, *args)
    r = _run(nc, [arrays], core_ids=[0])
    return r.results[0]["out_0_dram"]
```

```python
from contextlib import ExitStack

import concourse.bass as bass
from concourse import mybir

F32 = mybir.dt.float32
BF16 = mybir.dt.bfloat16
I32 = mybir.dt.int32
U32 = mybir.dt.uint32
ALU = mybir.AluOpType
ACT = mybir.ActivationFunctionType
AX_X = mybir.AxisListType.X
P = 128
EPS = 1e-5
BLK = 64
BEAT = 4
TURN = 8
FFN1 = [(0, 1), (1, 1), (2, 2), (4, 4)]
FFN2 = [(0, 2), (2, 2), (4, 2), (6, 1), (7, 1)]
X0 = [0, 8, 16, 0, 0, 16, 0, 16, 24]
TURNING = ("turn", "turn2", "hadd", "proj")


class Chunk:
    pass


class Beat:
    def __init__(self, at):
        self.at, self.tile, self.steps, self.side = at, None, [], []


def plan_chunks(JB, E):
    chunks, g0, q0, m0 = [], 0, 0, 0
    for i, (blk, nblk) in enumerate(FFN1 + FFN2):
        c = Chunk()
        c.index, c.blk, c.nblk, c.second = i, blk, nblk, i >= len(FFN1)
        c.n0, c.J = blk * JB, nblk * JB
        c.S = c.J + E - 1
        c.NP = (c.S + 1) // 2
        c.g0, c.q0, c.m0, c.region = g0, q0, m0, i % 2
        c.x0 = X0[i]
        g0, q0, m0 = g0 + c.S, q0 + c.NP, m0 + c.J
        chunks.append(c)
    return chunks


def plan_beats(chunks, NBLK, T, ZS):
    TILE, STEP, ROW, LATENCY = 2.35, 0.9, 1.1, 2.8
    beats, sp = [], []
    ready_beat, bias_beat = {}, {}
    jobs = []

    def routing(c):
        n = range(c.J // TURN)
        return ([("stats", c, i) for i in n] + [("root", c)] + [("norm", c, i) for i in n] + [("turn", c, i) for i in n]
                + [("logits", c), ("pick", c), ("rank", c), ("slots", c)])

    cost = {"stats": 2.1, "root": 2.6, "norm": 1.2, "turn": 1.4, "logits": 0, "pick": 1.3, "rank": 0, "slots": 2.8,
            "proj": 1.4, "add": 1.2, "stats2": 2.1, "root2": 2.6, "norm2": 1.2, "turn2": 1.4, "hadd": 1.4, "bias": 0.7,
            "xi0": 0}
    first = routing(chunks[0])
    jobs.append([0, first])
    jobs.append([1, [("proj", None, i) for i in range(4)], 6])
    for c in chunks[1:len(FFN1)]:
        jobs.append([2 + c.index, routing(c)])
    now, pool_free = 0.0, 0.0
    t, tiles = 0, [(c, k) for c in chunks for k in range(c.S)]
    at_tile = 0
    ready = {}
    back_at = {}
    asked_gather, done_add = 0, set()
    inputs_ready = set()
    beat_of_tile = {}
    waiting_bias = asked_bias = None
    requests = []
    routed_order = []
    hadd_asked = set()
    next_route = 0
    gathers = [(c, b) for c in chunks for b in range(c.nblk)]
    while at_tile < len(tiles) or t < T or jobs or asked_gather < len(gathers) or len(done_add) < len(gathers):
        b = Beat(len(beats))
        if at_tile < len(tiles):
            c, k = tiles[at_tile]
            if c.index in ready and now >= ready[c.index] and (k or b.at >= ready_beat[c.index] + 1):
                b.tile = (c, k)
                beat_of_tile[c.g0 + k] = b.at
                at_tile += 1
        while t < T and len(b.steps) < (3 if b.tile else BEAT):
            zc, s = divmod(t, ZS)
            more = zc + 1 < T // ZS
            if bias_beat.get(zc, b.at) >= b.at or s == 4 and more and (zc + 1) * ZS // BLK not in inputs_ready:
                break
            b.steps.append(t)
            t += 1
            if s == 7 and more:
                waiting_bias, asked_bias = zc + 1, b.at
        room = (1.6 if b.tile and b.steps else 3.4 if b.steps else 1.4 if b.tile else 4.5)
        if waiting_bias is not None and asked_bias < b.at:
            b.side.append(("bias", None, waiting_bias))
            bias_beat[waiting_bias] = b.at
            waiting_bias = asked_bias = None
            room -= 0.7
        turned = False
        for job in sorted(jobs, key=lambda j: j[0]):
            if not job[1]:
                continue
            piece = job[1][0]
            if job[2:] and b.at < job[2]:
                continue
            if piece[0] in TURNING and turned:
                continue
            if cost[piece[0]] > room and b.side:
                continue
            if piece[0] in ("stats", "root", "norm", "turn", "logits", "pick", "rank", "slots"):
                if piece[1].index != next_route:
                    continue
                if piece[0] == "slots" and 2 <= piece[1].index < len(FFN1) and asked_gather < piece[1].index - 1:
                    continue
            job[1].pop(0)
            b.side.append(piece)
            room -= cost[piece[0]]
            turned = turned or piece[0] in TURNING
            if piece[0] == "slots":
                c = piece[1]
                next_route += 1
                start = max(pool_free, now + 4.0)
                pool_free = start + c.J * ROW
                ready[c.index] = pool_free + LATENCY
                ready_beat[c.index] = b.at
                requests.append(("scatter", c))
            if piece[0] == "turn2":
                inputs_ready.add(piece[1])
                if piece[1] == 0:
                    jobs.append([0, [("xi0", None, 0)], b.at + 1])
            if piece[0] == "xi0":
                waiting_bias, asked_bias = 0, b.at
            if piece[0] == "add":
                done_add.add(piece[1])
                if piece[1] >= NBLK:
                    sp.append((b.at + 0.5, "out", piece[1] - NBLK))
        jobs = [j for j in jobs if j[1]]
        now += (max((TILE if b.tile else 0) + 0.12 * len(b.steps), STEP * len(b.steps),
                    (1.1 if b.tile else 0) + sum(cost[p[0]] for p in b.side), 0.3))
        while asked_gather < len(gathers):
            c, bl = gathers[asked_gather]
            last = beat_of_tile.get(c.g0 + c.S - 1)
            if last is None or b.at < last + 2 or (asked_gather >= 4 and asked_gather - 4 not in done_add):
                break
            start = max(pool_free, now + LATENCY)
            pool_free = start + (c.J // c.nblk) * ROW
            back_at[asked_gather] = pool_free + LATENCY
            requests.append(("gather", c, bl, asked_gather))
            asked_gather += 1
        for n in list(back_at):
            if now >= back_at[n]:
                del back_at[n]
                if n < NBLK:
                    jobs.append([n, [("add", n), ("stats2", n, 0), ("root2", n), ("norm2", n), ("turn2", n, 0)], b.at + 1])
                else:
                    jobs.append([9, [("add", n)], b.at + 1])
        for blk in range(NBLK):
            if t >= (blk + 1) * BLK and blk not in hadd_asked:
                hadd_asked.add(blk)
                c = next(c for c in chunks if c.second and c.blk <= blk < c.blk + c.nblk)
                jobs.append([1.5 + blk, [("hadd", blk, 0)] + (routing(c) if blk == c.blk + c.nblk - 1 else []), b.at + 1])
        beats.append(b)
    return beats, requests, sp, beat_of_tile, ready_beat



def build(nc, x, Wi, bi, Wh, bh, router_w, expert_fc, expert_proj, out):
    B, T, D = x.shape
    E, _, HD = expert_fc.shape
    HC = HD // P
    TH = P // B
    NBLK = T // BLK
    JB = BLK // TH
    NT = NBLK * JB
    ZS = 512 // B

    chunks = plan_chunks(JB, E)
    JMAX = max(c.J for c in chunks)
    TMAX = JMAX + E
    beats, pool_dmas, outs, beat_of_tile, ready_beat = plan_beats(chunks, NBLK, T, ZS)
    tile_at = lambda n: beats[n].tile if 0 <= n < len(beats) else None

    with ExitStack() as ctx:
        def sb(name, shape, dt=F32):
            return ctx.enter_context(nc.sbuf_tensor(name, shape, dt))

        def psum(name):
            return ctx.enter_context(nc.psum_tensor(name, [P, 512], F32))

        def sem(name):
            return ctx.enter_context(nc.semaphore(name))

        xs_dram = [nc.dram_tensor(f"xs_dram{i}", [TMAX * P, D], F32).ap() for i in range(2)]
        ys_dram = [nc.dram_tensor(f"ys_dram{i}", [TMAX * P, D], F32).ap() for i in range(2)]

        x_sb = sb("x_sb", [P, NT, D])
        xnf = sb("xnf", [P, JMAX, D])
        xns = sb("xns", [P, JB, D])
        back = sb("back", [P, 4, JB, D])
        xnT = sb("xnT", [P, 4, JB, P])
        hsT = sb("hsT", [P, (T + 1) * B])
        fc_sb = sb("fc_sb", [P, E * HD])
        projT = sb("projT", [P, E * HC * D])
        proj_raw = back[:, :, :, :].rearrange("p a b c -> p (a b c)")[:, 0:E * HD].rearrange("p (e h) -> p e h", e=E)
        w_raw = sb("w_raw", [P, 2, D])
        rw_raw = sb("rw_raw", [E, D])
        wT = sb("wT", [P, 2 * P + E])
        WiT, WhT, rwT = wT[:, 0:P], wT[:, P:2 * P], wT[:, 2 * P:2 * P + E]
        bias2 = sb("bias2", [P, 2])
        bias = sb("bias", [P, 1])
        ident = sb("ident", [P, P])
        before = sb("before", [P, P], BF16)
        ones = sb("ones", [P, P], BF16)
        zeros = sb("zeros", [P, 512])
        kio_i = sb("kio_i", [P, 64], I32)
        kio = sb("kio", [P, 64])
        thr = sb("thr", [P, JMAX])
        pref = sb("pref", [P, E])
        lower = sb("lower", [P, E, E])
        warm = sb("warm", [P, 1])
        stats = sb("stats", [P, 2, JMAX, 6])
        mv = sb("mv", [P, 2, JMAX, 2])
        rstd = sb("rstd", [P, 2, JMAX])
        var_eps = sb("var_eps", [P, JMAX])
        newton = sb("newton", [P, JMAX])
        root_bits = sb("root_bits", [P, JMAX], I32)
        xrt = sb("xrt", [P, 2, 512])
        best = sb("best", [P, JMAX])
        eq = sb("eq", [P, JMAX, E])
        wgt = sb("wgt", [P, JMAX, E])
        oh = sb("oh", [P, JMAX, E], BF16)
        cmp = sb("cmp", [P, E, JMAX])
        ntile = sb("ntile", [P, E])
        tmp8 = sb("tmp8", [P, E, E])
        first_tile = sb("first_tile", [P, E])
        end_tile = sb("end_tile", [P, E])
        posw = sb("posw", [P, JMAX, E])
        posf = sb("posf", [P, JMAX])
        pos = sb("pos", [P, len(chunks), JMAX], I32)
        cmp2 = sb("cmp2", [P, TMAX, E])
        exf = sb("exf", [P, TMAX])
        eoff = sb("eoff", [P, len(chunks), TMAX], I32)
        xs_sb = sb("xs_sb", [P, 4, D])
        xT_sb = sb("xT_sb", [P, 2, P])
        r_sb = sb("r_sb", [P, 2, HD])
        s_sb = sb("s_sb", [P, 2, HC, P])
        y_sb = sb("y_sb", [P, 4, D])

        z = ctx.enter_context(nc.psum_tensor("z", [P, 2, 512], F32))
        mT = psum("mT")
        xTp, hp, rTp, yp, lg = psum("xTp"), psum("hp"), psum("rTp"), psum("yp"), psum("lg")

        s_in = [sem(f"s_in{i}") for i in range(NBLK)]
        s_w = sem("s_w")
        s_fc = sem("s_fc")
        s_pr = sem("s_pr")
        s_const = sem("s_const")
        s_kc = sem("s_kc")
        s_zero = sem("s_zero")
        s_dve = sem("s_dve")
        s_tr = sem("s_tr")
        s_evac = sem("s_evac")
        s_xnf = sem("s_xnf")
        s_xns = sem("s_xns")
        s_rt = sem("s_rt")
        s_oh = sem("s_oh")
        s_rank = sem("s_rank")
        s_pos = sem("s_pos")
        s_eoff = sem("s_eoff")
        s_scat = [sem(f"s_scat{i}") for i in range(len(chunks))]
        s_gath = [sem(f"s_gath{i}") for i in range(2 * NBLK)]
        s_add = sem("s_add")
        s_load = sem("s_load")
        s_t0 = sem("s_t0")
        s_xt = sem("s_xt")
        s_m1 = sem("s_m1")
        s_relu = sem("s_relu")
        s_rtr = sem("s_rtr")
        s_sq = sem("s_sq")
        s_m2 = sem("s_m2")
        s_y = sem("s_y")
        s_store = sem("s_store")
        s_xi = sem("s_xi")
        s_z = sem("s_z")
        s_mm = sem("s_mm")
        s_h = sem("s_h")
        s_out = sem("s_out")

        block = ctx.enter_context(nc.Block())

        def tokens(dram, blk):
            return dram[:, blk * BLK:(blk + 1) * BLK, :].rearrange("b (th j) d -> th b (j d)", th=TH)

        def sb_block(blk):
            return x_sb[:, blk * JB:(blk + 1) * JB, :].rearrange("p j d -> p (j d)")

        def state(t):
            blk, r = divmod(t, BLK)
            th, j = divmod(r, JB)
            at = B + blk * BLK * B + j * P + th * B
            return hsT[:, at:at + B]

        def z_step(t):
            zc, s = divmod(t, ZS)
            return z[:, zc % 2, s * B:(s + 1) * B]

        def pair(c, k):
            return c.q0 + k // 2

        def buf(c, k):
            return pair(c, k) % 2 * 2 + k % 2

        def tiles_before(c, q):
            return c.g0 + min(2 * q + 2, c.S)

        def gather_number(c, bl):
            return (NBLK if c.second else 0) + c.blk + bl

        @block.sync
        def _(sp):
            sp.dma_start(sb_block(0), tokens(x, 0)).then_inc(s_in[0], 16)
            sp.dma_start(rw_raw[:, :], router_w).then_inc(s_w, 16)
            sp.dma_start(w_raw[:, 0, :], Wi).then_inc(s_w, 16)
            sp.dma_start(w_raw[:, 1, :], Wh).then_inc(s_w, 16)
            sp.dma_start(bias2[:, 0:1], bi.rearrange("(p a) -> p a", a=1)).then_inc(s_w, 16)
            sp.dma_start(bias2[:, 1:2], bh.rearrange("(p a) -> p a", a=1)).then_inc(s_w, 16)
            sp.dma_start(proj_raw, expert_proj.rearrange("e d h -> d e h")).then_inc(s_pr, 16)
            sp.dma_start(sb_block(1), tokens(x, 1)).then_inc(s_in[1], 16)
            sp.wait_ge(s_const, 1)
            for i in range(2):
                sp.dma_start(xs_dram[i].rearrange("(p r c) d -> p r (c d)", p=P, c=4),
                             zeros[:, :].unsqueeze(1).to_broadcast([P, TMAX // 4, 512])).then_inc(s_zero, 16)
            sp.dma_start(fc_sb[:, :].rearrange("p (e h) -> p e h", e=E),
                         expert_fc.rearrange("e d h -> d e h")).then_inc(s_fc, 16)
            for blk in range(2, NBLK):
                sp.dma_start(sb_block(blk), tokens(x, blk)).then_inc(s_in[blk], 16)

            def load(c, q):
                Q = c.q0 + q
                sp.wait_ge(s_scat[c.index], 16 * c.J)
                if Q:
                    sp.wait_ge(s_load, 16 * Q)
                if Q >= 2:
                    d, r = (c, q - 2) if q >= 2 else (chunks[c.index - 1], chunks[c.index - 1].NP - 2 + q)
                    sp.wait_ge(s_t0, tiles_before(d, r))
                sp.dma_start(xs_sb[:, Q % 2 * 2:Q % 2 * 2 + 2, :],
                             xs_dram[c.region][2 * q * P:2 * (q + 1) * P, :].rearrange("(a p) d -> p a d", p=P)
                             ).then_inc(s_load, 16)

            def store(c, q):
                Q, n = c.q0 + q, min(2, c.S - 2 * q)
                sp.wait_ge(s_y, tiles_before(c, q))
                if Q:
                    sp.wait_ge(s_store, 16 * Q)
                if q == 0 and c.index >= 2:
                    for bl in range(chunks[c.index - 2].nblk):
                        sp.wait_ge(s_gath[gather_number(chunks[c.index - 2], bl)], 16 * JB)
                sp.dma_start(ys_dram[c.region][2 * q * P:(2 * q + n) * P, :].rearrange("(a p) d -> p a d", p=P),
                             y_sb[:, Q % 2 * 2:Q % 2 * 2 + n, :]).then_inc(s_store, 16)

            dmas = [(at, "out", blk, None) for at, _, blk in outs]
            for c in chunks:
                for q in range(c.NP):
                    start = beat_of_tile[c.g0] - 2.2
                    if c.q0 + q >= 2:
                        d, r = (c, q - 2) if q >= 2 else (chunks[c.index - 1], chunks[c.index - 1].NP - 2 + q)
                        start = max(start, beat_of_tile[tiles_before(d, r) - 1] - 0.5)
                    dmas.append((start, "load", c, q))
                    dmas.append((beat_of_tile[tiles_before(c, q) - 1] + 1.2, "store", c, q))
            for at, what, c, q in sorted(dmas, key=lambda d: d[0]):
                if what == "load":
                    load(c, q)
                elif what == "store":
                    store(c, q)
                else:
                    sp.wait_ge(s_add, NBLK + c + 1)
                    sp.dma_start(tokens(out, c), sb_block(c)).then_inc(s_out, 16)
            sp.wait_ge(s_zero, 32)
            sp.wait_ge(s_store, 16 * (chunks[-1].q0 + chunks[-1].NP))
            sp.wait_ge(s_out, 16 * NBLK)

        @block.gpsimd
        def _(pool):
            pool.memset(zeros[:, :], 0.0).then_inc(s_const, 1)
            pool.memset(hsT[:, 0:B], 0.0).then_inc(s_const, 1)
            pool.memset(ident[:, :], 0.0).then_inc(s_const, 1)
            pool.memset(before[:, :], 1.0).then_inc(s_const, 1)
            pool.memset(ones[:, :], 1.0).then_inc(s_const, 1)
            pool.iota(kio_i[:, :], pattern=[[1, 64]], base=0, channel_multiplier=0).then_inc(s_const, 1)
            pool.wait_ge(s_const, 6)
            pool.affine_select(out=ident[:, :], in_=ident[:, :], compare_op=ALU.not_equal, fill=1.0, base=0,
                               pattern=[[-1, P]], channel_multiplier=1).then_inc(s_const, 1)
            pool.affine_select(out=before[:, :], in_=before[:, :], compare_op=ALU.is_gt, fill=0.0, base=0,
                               pattern=[[1, P]], channel_multiplier=-1).then_inc(s_const, 1)

            def scatter(c):
                pool.wait_ge(s_pos, c.index + 1)
                pool.wait_ge(s_xnf, c.m0 + c.J)
                if c.index == 0:
                    pool.wait_ge(s_zero, 32)
                if c.index >= 2:
                    d = chunks[c.index - 2]
                    pool.wait_ge(s_load, 16 * (d.q0 + d.NP))
                for j in range(c.J):
                    pool.indirect_dma_start(
                        out=xs_dram[c.region], in_=xnf[:, c.x0 + j, :], in_offset=None,
                        out_offset=bass.IndirectOffsetOnAxis(ap=pos[:, c.index, j:j + 1].bitcast(U32), axis=0),
                    ).then_inc(s_scat[c.index], 16)

            def gather(c, bl, n):
                pool.wait_ge(s_store, 16 * (c.q0 + c.NP))
                if n >= 4:
                    pool.wait_ge(s_add, n - 3)
                for j in range(JB):
                    pool.indirect_dma_start(
                        out=back[:, n % 4, j, :], out_offset=None, in_=ys_dram[c.region][0:c.S * P, :],
                        in_offset=bass.IndirectOffsetOnAxis(ap=pos[:, c.index, bl * JB + j:bl * JB + j + 1].bitcast(U32), axis=0)
                    ).then_inc(s_gath[n], 16)

            for what in pool_dmas:
                if what[0] == "scatter":
                    scatter(what[1])
                else:
                    gather(*what[1:])

        @block.vector
        def _(dve):
            count = {"chain": 0, "groups": 0}
            hadd_groups = {}

            def link(ins):
                count["chain"] += 1
                ins.then_inc(s_dve, 1)
                dve.wait_ge(s_dve, count["chain"])

            def evacuate(op, out_ap, *ins):
                count["groups"] += 1
                dve.wait_ge(s_tr, count["groups"])
                op(out_ap, *ins).then_inc(s_evac, 1)

            def statistics(w, n0, tiles):
                for j in tiles:
                    dve.bn_stats(stats[:, w, j, :], x_sb[:, n0 + j, :]).then_inc(s_dve, 1)
                count["chain"] += len(tiles)
                dve.wait_ge(s_dve, count["chain"])
                for j in tiles:
                    dve.bn_aggr(mv[:, w, j, :], stats[:, w, j, :]).then_inc(s_dve, 1)
                count["chain"] += len(tiles)

            def inverse_root(w, J):
                v, y, t, r = var_eps[:, 0:J], rstd[:, w, 0:J], newton[:, 0:J], root_bits[:, 0:J]
                dve.wait_ge(s_dve, count["chain"])
                link(dve.tensor_scalar(v, mv[:, w, 0:J, 1], EPS, None, ALU.add))
                link(dve.tensor_scalar(r, v.bitcast(I32), 1, None, ALU.arith_shift_right))
                link(dve.tensor_scalar(y.bitcast(I32), r, -1.0, float(0x5F3759DF), ALU.mult, ALU.add))
                for _ in range(4):
                    link(dve.tensor_tensor(t, y, y, ALU.mult))
                    link(dve.scalar_tensor_tensor(out=t, in0=t, scalar=-0.5, in1=v, op0=ALU.mult, op1=ALU.mult))
                    link(dve.scalar_tensor_tensor(out=y, in0=t, scalar=1.5, in1=y, op0=ALU.add, op1=ALU.mult))

            def normalise(w, n0, tiles, dst, x0, done):
                for j in tiles:
                    dve.tensor_scalar(dst[:, x0 + j, :], x_sb[:, n0 + j, :], mv[:, w, j, 0:1], rstd[:, w, j:j + 1],
                                      ALU.subtract, ALU.mult).then_inc(done, 1)

            def pick(c):
                J = c.J
                lg3 = lg[:, 0:J * E].rearrange("p (j e) -> p j e", e=E)
                dve.wait_ge(s_rt, (c.m0 + J) // 4)
                link(dve.tensor_reduce(best[:, 0:J], lg3, AX_X, ALU.max))
                link(dve.tensor_tensor(eq[:, 0:J, :], lg3, best[:, 0:J].unsqueeze(2).to_broadcast([P, J, E]), ALU.is_ge))
                link(dve.tensor_tensor(wgt[:, 0:J, :], eq[:, 0:J, :], pref[:, :].unsqueeze(1).to_broadcast([P, J, E]), ALU.mult))
                link(dve.tensor_reduce(best[:, 0:J], wgt[:, 0:J, :], AX_X, ALU.max))
                dve.tensor_tensor(oh[:, 0:J, :], wgt[:, 0:J, :], best[:, 0:J].unsqueeze(2).to_broadcast([P, J, E]),
                                  ALU.is_equal).then_inc(s_oh, 1)

            def slots(c):
                J, S = c.J, c.S
                rk3 = lg[:, 0:(J + 1) * E].rearrange("p (j e) -> p j e", e=E)
                dve.wait_ge(s_rank, c.index + 1)
                link(dve.tensor_tensor(cmp[:, :, 0:J], rk3[:, J, :].unsqueeze(2).to_broadcast([P, E, J]),
                                       thr[:, 0:J].unsqueeze(1).to_broadcast([P, E, J]), ALU.is_gt))
                link(dve.tensor_reduce(ntile[:, :], cmp[:, :, 0:J], AX_X, ALU.add))
                link(dve.tensor_tensor(tmp8[:, :, :], lower[:, :, :], ntile[:, :].unsqueeze(1).to_broadcast([P, E, E]), ALU.mult))
                link(dve.tensor_reduce(first_tile[:, :], tmp8[:, :, :], AX_X, ALU.add))
                dve.tensor_tensor(end_tile[:, :], first_tile[:, :], ntile[:, :], ALU.add).then_inc(s_dve, 1)
                count["chain"] += 1
                link(dve.scalar_tensor_tensor(out=posw[:, 0:J, :], in0=first_tile[:, :].unsqueeze(1).to_broadcast([P, J, E]),
                                              scalar=float(P), in1=rk3[:, 0:J, :], op0=ALU.mult, op1=ALU.add))
                link(dve.tensor_tensor(posw[:, 0:J, :], posw[:, 0:J, :], oh[:, 0:J, :], ALU.mult))
                link(dve.tensor_reduce(posf[:, 0:J], posw[:, 0:J, :], AX_X, ALU.add))
                dve.tensor_scalar(pos[:, c.index, 0:J], posf[:, 0:J], float(S * P - 1), None, ALU.min).then_inc(s_pos, 1)
                link(dve.tensor_tensor(cmp2[:, 0:S, :], kio[:, 0:S].unsqueeze(2).to_broadcast([P, S, E]),
                                       end_tile[:, :].unsqueeze(1).to_broadcast([P, S, E]), ALU.is_ge))
                link(dve.tensor_reduce(exf[:, 0:S], cmp2[:, 0:S, :], AX_X, ALU.add))
                dve.tensor_scalar(eoff[:, c.index, 0:S], exf[:, 0:S], float(E - 1), float(HD), ALU.min, ALU.mult
                                  ).then_inc(s_eoff, 1)

            def copy_xT(c, k):
                g = c.g0 + k
                dve.wait_ge(s_t0, g + 1)
                if g >= 2:
                    dve.wait_ge(s_m1, g - 1)
                dve.tensor_copy(xT_sb[:, g % 2, :], xTp[:, 0:P]).then_inc(s_xt, 1)

            def relu(c, k):
                g = c.g0 + k
                dve.wait_ge(s_m1, g + 1)
                if g >= 2:
                    dve.wait_ge(s_rtr, g - 1)
                dve.tensor_scalar(r_sb[:, g % 2, :], hp[:, :], 0.0, None, ALU.max).then_inc(s_relu, 1)

            def halve(c, k):
                dve.wait_ge(s_m2, c.g0 + k + 1)
                if pair(c, k) >= 2 and k % 2 == 0:
                    dve.wait_ge(s_store, 16 * (pair(c, k) - 1))
                dve.tensor_scalar(y_sb[:, buf(c, k), :], yp[:, 0:D], 0.5, None, ALU.mult).then_inc(s_y, 1)

            def turned(what, c, i, g):
                n = 2 * i + g
                if what == "turn":
                    if c.m0 // 4 + n >= 2:
                        dve.wait_ge(s_rt, c.m0 // 4 + n - 1)
                    evacuate(dve.tensor_copy, xrt[:, n % 2, :], mT[:, :])
                elif what == "turn2":
                    if c >= 4 and n == 0:
                        dve.wait_ge(s_xi, (c - 3) * (BLK // ZS))
                    evacuate(dve.tensor_copy, xnT[:, c % 4, 4 * n:4 * n + 4, :].rearrange("p j t -> p (j t)"), mT[:, :])
                elif what == "hadd":
                    v = x_sb[:, c * JB + 4 * n:c * JB + 4 * n + 4, :].rearrange("p j d -> p (j d)")
                    count["groups"] += 1
                    dve.wait_ge(s_tr, count["groups"])
                    dve.tensor_tensor(v, v, mT[:, :], ALU.add).then_inc(s_evac, 1)
                    hadd_groups[c] = count["groups"]
                else:
                    evacuate(dve.tensor_copy, projT[:, n * 512:(n + 1) * 512], mT[:, :])

            def other(what, c, i):
                if what == "stats":
                    if c.second:
                        dve.wait_ge(s_evac, hadd_groups[c.blk + i])
                    else:
                        dve.wait_ge(s_in[c.blk + i], 16)
                    statistics(0, c.n0, range(8 * i, 8 * i + 8))
                elif what == "root":
                    inverse_root(0, c.J)
                elif what == "norm":
                    if i == 0:
                        for d in chunks[max(c.index - 3, 0):c.index]:
                            if d.x0 < c.x0 + c.J and c.x0 < d.x0 + d.J:
                                dve.wait_ge(s_scat[d.index], 16 * d.J)
                    normalise(0, c.n0, range(TURN * i, TURN * (i + 1)), xnf, c.x0, s_xnf)
                elif what == "pick":
                    pick(c)
                elif what == "slots":
                    slots(c)
                elif what == "add":
                    dve.wait_ge(s_gath[c], 16 * JB)
                    v = sb_block(c % NBLK)
                    dve.tensor_tensor(v, v, back[:, c % 4, :, :].rearrange("p j d -> p (j d)"), ALU.add).then_inc(s_add, 1)
                elif what == "stats2":
                    dve.wait_ge(s_add, c + 1)
                    statistics(1, c * JB, range(8 * i, 8 * i + 8))
                elif what == "root2":
                    inverse_root(1, JB)
                elif what == "norm2":
                    normalise(1, c * JB, range(JB), xns, 0, s_xns)
                elif what == "bias":
                    dve.wait_ge(s_xi, i + 1)
                    zb = z[:, i % 2, :]
                    dve.tensor_scalar(zb, zb, bias[:, 0:1], None, ALU.add).then_inc(s_z, 1)

            dve.wait_ge(s_const, 8)
            link(dve.tensor_copy(kio[:, :], kio_i[:, :]))
            dve.tensor_scalar(thr[:, :], kio[:, 0:JMAX], float(P), None, ALU.mult).then_inc(s_kc, 1)
            dve.tensor_scalar(pref[:, :], kio[:, 0:E], -1.0, float(E), ALU.mult, ALU.add).then_inc(s_kc, 1)
            dve.tensor_tensor(lower[:, :, :], kio[:, 0:E].unsqueeze(1).to_broadcast([P, E, E]),
                              kio[:, 0:E].unsqueeze(2).to_broadcast([P, E, E]), ALU.is_lt).then_inc(s_kc, 1)
            dve.wait_ge(s_w, 80)
            dve.tensor_tensor(bias[:, :], bias2[:, 0:1], bias2[:, 1:2], ALU.add).then_inc(s_kc, 1)
            dve.wait_ge(s_kc, 4)
            evacuate(dve.tensor_copy, wT[:, :], mT[:, 0:2 * P + E])

            for b in beats:
                now, after, last = b.tile, tile_at(b.at + 1), tile_at(b.at - 1)
                turning = [p for p in b.side if p[0] in TURNING]
                for p in turning:
                    turned(*p, 0)
                if now:
                    relu(*now)
                if after:
                    copy_xT(*after)
                for p in turning:
                    turned(*p, 1)
                if last:
                    halve(*last)
                for p in b.side:
                    if p[0] not in TURNING:
                        other(*(p + (None,))[:3])

        @block.scalar
        def _(act):
            act.wait_ge(s_const, 1)
            act.activation(warm[:, :], zeros[:, 0:1], ACT.Tanh)

            def tanh(t):
                act.wait_ge(s_mm, t + 1)
                act.activation(state(t), z_step(t), ACT.Tanh).then_inc(s_h, 1)

            def square(c, k, half):
                g, w = c.g0 + k, HC // 2
                if half == 0:
                    act.wait_ge(s_rtr, g + 1)
                    if g >= 2:
                        act.wait_ge(s_m2, g - 1)
                act.activation(s_sb[:, g % 2, half * w:(half + 1) * w, :].rearrange("p c t -> p (c t)"),
                               rTp[:, half * w * P:(half + 1) * w * P], ACT.Square).then_inc(s_sq, 1)

            for b in beats:
                last = tile_at(b.at - 1)
                for i in range(BEAT):
                    if i < len(b.steps):
                        tanh(b.steps[i])
                    if last and i < 2:
                        square(*last, i)

        @block.tensor
        def _(pe):
            groups = [0]
            offsets = {}

            def transpose4(ins):
                if groups[0]:
                    pe.wait_ge(s_evac, groups[0])
                groups[0] += 1
                at = 0
                for a in ins:
                    rows = a.shape[0]
                    last = pe.transpose(mT[:, at:at + rows], a, ident[0:rows, 0:rows])
                    at += rows
                last.then_inc(s_tr, 1)

            def logits(c, n):
                if n == 0 and c.index:
                    pe.wait_ge(s_eoff, c.index)
                pe.wait_ge(s_evac, turn_at[n])
                for q in range(4):
                    j = 4 * n + q
                    mm = pe.matmul(lg[:, j * E:(j + 1) * E], xrt[:, n % 2, q * P:(q + 1) * P], rwT, start=True, stop=True)
                mm.then_inc(s_rt, 1)

            turn_at, xnT_at = {}, {}

            def turn(what, c, i, g):
                n = 2 * i + g
                if what == "turn":
                    if i:
                        logits(c, n - 2)
                    pe.wait_ge(s_xnf, c.m0 + 4 * n + 4)
                    transpose4([xnf[:, c.x0 + 4 * n + q, :] for q in range(4)])
                    turn_at[n] = groups[0]
                elif what == "turn2":
                    pe.wait_ge(s_xns, c * JB + 4 * n + 4)
                    transpose4([xns[:, 4 * n + q, :] for q in range(4)])
                    xnT_at[c] = groups[0]
                elif what == "hadd":
                    pe.wait_ge(s_h, (c + 1) * BLK)
                    at = B + c * BLK * B + 4 * n * P
                    transpose4([hsT[:, at + q * P:at + (q + 1) * P] for q in range(4)])
                else:
                    pe.wait_ge(s_pr, 16)
                    transpose4([proj_raw[:, n, h * P:(h + 1) * P] for h in range(HC)])

            def rank(c):
                pe.wait_ge(s_oh, c.index + 1)
                n = c.J * E
                ohc = oh[:, 0:c.J, :].rearrange("p j e -> p (j e)")
                pe.matmul(lg[:, 0:n], before[:, :], ohc, start=True, stop=False, skip_group_check=True)
                for s in range(1, c.J + 1):
                    mm = pe.matmul(lg[:, s * E:n + E], ones[:, :], ohc[:, 0:n + E - s * E], start=False,
                                   stop=(s == c.J), skip_group_check=True)
                mm.then_inc(s_rank, 1)

            def load_offset(c, k):
                if k == 0:
                    pe.wait_ge(s_eoff, c.index + 1)
                offsets[c.g0 + k] = nc.values_load(eoff[0:1, c.index, k:k + 1], engines=[mybir.EngineType.PE], min_val=0,
                                                   max_val=(E - 1) * HD, skip_runtime_bounds_check_because="clamped where it is computed")

            def turn_x(c, k):
                g = c.g0 + k
                pe.wait_ge(s_load, 16 * (pair(c, k) + 1))
                if g:
                    pe.wait_ge(s_xt, g)
                pe.transpose(xTp[:, 0:P], xs_sb[:, buf(c, k), :], ident[:, :]).then_inc(s_t0, 1)

            def product1(c, k, half):
                g = c.g0 + k
                if half == 0:
                    if g == 0:
                        pe.wait_ge(s_fc, 16)
                    pe.wait_ge(s_xt, g + 1)
                    if g:
                        pe.wait_ge(s_relu, g)
                w = HD // 2
                mm = pe.matmul(hp[:, half * w:(half + 1) * w], xT_sb[:, g % 2, :], fc_sb[:, bass.ds(offsets[g] + half * w, w)],
                               start=True, stop=True)
                if half:
                    mm.then_inc(s_m1, 1)

            def turn_r(c, k):
                g = c.g0 + k
                pe.wait_ge(s_relu, g + 1)
                if g:
                    pe.wait_ge(s_sq, 2 * g)
                for h in range(HC):
                    mm = pe.transpose(rTp[:, h * P:(h + 1) * P], r_sb[:, g % 2, h * P:(h + 1) * P], ident[:, :])
                mm.then_inc(s_rtr, 1)

            def product2(c, k, h):
                g = c.g0 + k
                if h % 2 == 0:
                    pe.wait_ge(s_sq, 2 * g + 1 + h // 2)
                if h == 0 and g:
                    pe.wait_ge(s_y, g)
                mm = pe.matmul(yp[:, 0:D], s_sb[:, g % 2, h, :], projT[:, bass.ds(offsets[g] + h * D, D)],
                               start=(h == 0), stop=(h == HC - 1))
                if h == HC - 1:
                    mm.then_inc(s_m2, 1)

            def inputs(zc, q):
                blk, w = divmod(zc, BLK // ZS)
                if q == 0:
                    pe.wait_ge(s_evac, xnT_at[blk])
                th = w * (ZS // JB) + q
                mm = pe.matmul(z[:, zc % 2, q * P:(q + 1) * P], WiT, xnT[:, blk % 4, :, th * B:(th + 1) * B],
                               start=(q == 0), stop=False, skip_group_check=True)
                if q == 3:
                    mm.then_inc(s_xi, 1)

            def step(t):
                zc, s = divmod(t, ZS)
                if s == 0:
                    pe.wait_ge(s_z, zc + 1)
                if t:
                    pe.wait_ge(s_h, t)
                pe.matmul(z_step(t), WhT, state(t - 1), start=False, stop=True, skip_group_check=True).then_inc(s_mm, 1)
                if 4 <= s < 8 and zc + 1 < T // ZS:
                    inputs(zc + 1, s - 4)

            pe.wait_ge(s_const, 8)
            pe.wait_ge(s_w, 80)
            transpose4([w_raw[:, 0, :], w_raw[:, 1, :], rw_raw[:, :]])
            pe.wait_ge(s_evac, 1)

            for b in beats:
                now, after, last = b.tile, tile_at(b.at + 1), tile_at(b.at - 1)
                turning = [p for p in b.side if p[0] in TURNING]
                if len(b.steps) > 0:
                    step(b.steps[0])
                if now:
                    product1(*now, 0)
                for p in turning:
                    turn(*p, 0)
                if len(b.steps) > 1:
                    step(b.steps[1])
                if now:
                    product1(*now, 1)
                if after:
                    turn_x(*after)
                for p in turning:
                    turn(*p, 1)
                if len(b.steps) > 2:
                    step(b.steps[2])
                if last:
                    for h in range(3):
                        product2(*last, h)
                if len(b.steps) > 3:
                    step(b.steps[3])
                if last:
                    product2(*last, 3)
                if after:
                    load_offset(*after)
                if now:
                    turn_r(*now)
                for p in b.side:
                    if p[0] == "logits":
                        logits(p[1], p[1].J // 4 - 2)
                        logits(p[1], p[1].J // 4 - 1)
                    elif p[0] == "rank":
                        rank(p[1])
                    elif p[0] == "xi0":
                        for q in range(4):
                            inputs(0, q)


_INS = ['L0_attn_x', 'L0_attn_Wi', 'L0_attn_bi', 'L0_attn_Wh', 'L0_attn_bh', 'L0_ffn_router_w', 'L0_ffn_expert_fc',
        'L0_ffn_expert_proj']
_OUTS = [((16, 512, 128), 'float32')]


def kernel(**inputs):
    import numpy as _np
    import concourse.bacc as _bacc
    from concourse import mybir as _mybir
    from concourse.bass_utils import run_bass_kernel_spmd as _run

    nc = _bacc.Bacc("TRN2", target_bir_lowering=False, num_devices=1)
    arrays, args = {}, []
    for name in _INS:
        a = _np.ascontiguousarray(inputs[name])
        arrays[f"in_{name}_dram"] = a
        args.append(nc.dram_tensor(f"in_{name}_dram", a.shape, _mybir.dt.from_np(a.dtype), kind="ExternalInput").ap())
    for i, (shape, dtype) in enumerate(_OUTS):
        dt = _mybir.dt.from_np(_np.dtype(dtype))
        args.append(nc.dram_tensor(f"out_{i}_dram", shape, dt, kind="ExternalOutput").ap())
    build(nc, *args)
    r = _run(nc, [arrays], core_ids=[0])
    return r.results[0]["out_0_dram"]
```

```python
from contextlib import ExitStack

import concourse.bass as bass
from concourse import mybir

F32 = mybir.dt.float32
BF16 = mybir.dt.bfloat16
I32 = mybir.dt.int32
U32 = mybir.dt.uint32
ALU = mybir.AluOpType
ACT = mybir.ActivationFunctionType
AX_X = mybir.AxisListType.X
P = 128
EPS = 1e-5
BLK = 64
BEAT = 4
TURN = 8
FFNS = [(1, 0, 1), (1, 1, 1), (1, 2, 2), (1, 4, 2), (1, 6, 2), (2, 0, 2), (2, 2, 2), (2, 4, 2), (2, 6, 1), (2, 7, 1)]
X0 = [0, 8, 16, 0, 16, 0, 16, 0, 16, 24]
REGIONS = 3
XNF = 32
IN_BEATS = 2
PIECE = 4
TURNING = ("turn", "turn2", "hadd", "proj")


class Chunk:
    pass


class Beat:
    def __init__(self, at):
        self.at, self.tile, self.steps, self.side = at, None, [], []


def plan_chunks(JB, E):
    chunks, g0, q0, m0, b0 = [], 0, 0, 0, 0
    for i, (which, blk, nblk) in enumerate(FFNS):
        c = Chunk()
        c.index, c.blk, c.nblk, c.second = i, blk, nblk, which == 2
        c.n0, c.J = blk * JB, nblk * JB
        c.S = c.J + E - 1
        c.NP = (c.S + 1) // 2
        c.g0, c.q0, c.m0, c.b0, c.region = g0, q0, m0, b0, i % REGIONS
        c.x0 = X0[i]
        g0, q0, m0, b0 = g0 + c.S, q0 + c.NP, m0 + c.J, b0 + nblk
        chunks.append(c)
    return chunks


def plan_beats(chunks, NBLK, T, ZS):
    TILE, STEP, MM, ROW, LATENCY = 1.85, 0.68, 0.2, 1.05, 2.8
    NEAR = 11
    URGENT = 9.0
    cost = {"stats": (1.1, 0), "root": (1.2, 0), "norm": (0.6, 0), "turn": (1.3, 2.5), "logits": (0, 1.7), "pick": (1.3, 0),
            "rank": (0, 1.5), "slots": (2.0, 0), "experts": (0.8, 0), "proj": (1.3, 0.9), "add": (1.2, 0), "stats2": (1.1, 0),
            "root2": (1.2, 0), "norm2": (0.6, 0), "turn2": (1.3, 0.9), "hadd": (1.3, 0.9), "bias": (0.7, 0), "xi0": (0, 0.9)}
    ROUTING = ("stats", "root", "norm", "turn", "logits", "pick", "rank", "slots", "experts")

    def routing(c):
        n = range(c.J // PIECE)
        return ([("stats", c, i) for i in n] + [("root", c, 0), ("root", c, 1)] + [("norm", c, i) for i in n]
                + [("turn", c, i) for i in range(c.J // TURN)]
                + [("logits", c), ("pick", c), ("rank", c), ("slots", c), ("experts", c)])

    def recurrence(blk):
        n = range(TURN // PIECE)
        return ([("stats2", blk, i) for i in n] + [("root2", blk, 0), ("root2", blk, 1)] + [("norm2", blk, i) for i in n]
                + [("turn2", blk, 0)])

    beats, sp = [], []
    ready_beat, bias_beat = {}, {}

    def priority(job):
        if job[0] < 1:
            near = (10 * job[0] * BLK - ZS + 4 - t) / BEAT < NEAR
            return job[0] if near else 30 + job[0]
        return job[0]

    jobs = [[0, routing(chunks[0])], [1, [("proj", None, i) for i in range(4)], 6]]
    jobs += [[10 + c.index, routing(c)] for c in chunks[1:] if not c.second]
    now, pool_free = 0.0, 0.0
    t, at_tile, tiles = 0, 0, [(c, k) for c in chunks for k in range(c.S)]
    ready = {}
    back_at = {}
    gathers = [(c, i) for c in chunks for i in range(c.nblk)]
    asked_gather, next_route, next_add, next_norm = 0, 0, 0, 0
    inputs_ready, hadd_asked, beat_of_tile, requests = set(), set(), {}, []
    waiting_bias = asked_bias = None
    while at_tile < len(tiles) or t < T or jobs or asked_gather < len(gathers) or next_add < len(gathers):
        b = Beat(len(beats))
        if at_tile < len(tiles):
            c, k = tiles[at_tile]
            if c.index in ready_beat and now >= ready[c.index] and (k or b.at >= ready_beat[c.index] + 2):
                b.tile = (c, k)
                beat_of_tile[c.g0 + k] = b.at
                at_tile += 1
        while t < T and len(b.steps) < BEAT:
            zc, s = divmod(t, ZS)
            more = zc + 1 < T // ZS
            if bias_beat.get(zc, b.at) >= b.at or s == 4 and more and (zc + 1) * ZS // BLK not in inputs_ready:
                break
            b.steps.append(t)
            t += 1
            if s == 7 and more:
                waiting_bias, asked_bias = zc + 1, b.at
        room = (1.7 if b.tile and b.steps else 2.6 if b.steps else 1.0 if b.tile else 4.5)
        pe_side = dve_side = 0.0
        if waiting_bias is not None and asked_bias < b.at:
            b.side.append(("bias", None, waiting_bias))
            bias_beat[waiting_bias] = b.at
            waiting_bias = asked_bias = None
            dve_side += 0.7
        turned = False
        for job in sorted(jobs, key=priority):
            if job[2:] and b.at < job[2]:
                continue
            pieces = 0
            urgent = job[0] < 1 and not b.steps and job[0] * 10 <= (t + ZS - 4) // BLK
            while job[1] and pieces < (9 if urgent else 3):
                piece = job[1][0]
                on_dve, on_pe = cost[piece[0]]
                if piece[0] in TURNING and turned:
                    break
                if on_dve + dve_side > (URGENT if urgent else room) and b.side:
                    break
                if pieces and on_pe:
                    break
                if piece[0] in ROUTING:
                    c = piece[1]
                    if c.index > next_route + (piece[0] == "stats"):
                        break
                    if not at_tile and c.index and (c.index > 1 or piece[0] not in ("stats", "root", "norm") or b.at < 6):
                        break
                    if piece[0] == "slots" and c.index >= REGIONS and at_tile < chunks[c.index - REGIONS + 1].g0:
                        break
                    if piece[0] == "slots" and at_tile < len(tiles):
                        d = tiles[at_tile][0]
                        if d.index and not chunks[d.index - 1].second and asked_gather < d.b0:
                            break
                        if c.index >= d.index + 2 and not d.second and asked_gather < d.b0 + d.nblk and (
                                2.7 * (d.g0 + d.S - at_tile) < c.J * ROW):
                            break
                if piece[0] == "add" and piece[2] != gathers[next_add][0].blk + gathers[next_add][1]:
                    break
                if piece[0] == "stats2" and piece[1] != next_norm:
                    break
                job[1].pop(0)
                pieces += 1
                b.side.append(piece)
                dve_side += on_dve
                pe_side += on_pe
                turned = turned or piece[0] in TURNING
                if piece[0] == "slots":
                    start = max(pool_free, now + 3.0)
                    pool_free = start + c.J * ROW
                    ready[c.index] = pool_free + LATENCY + 2.2
                    requests.append(("scatter", c))
                elif piece[0] == "experts":
                    ready_beat[c.index] = b.at
                    next_route += 1
                elif piece[0] == "norm2" and piece[2]:
                    next_norm += 1
                elif piece[0] == "turn2":
                    inputs_ready.add(piece[1])
                    if piece[1] == 0:
                        jobs.append([0, [("xi0", None, 0)], b.at + 1])
                elif piece[0] == "xi0":
                    waiting_bias, asked_bias = 0, b.at
                elif piece[0] == "add":
                    next_add += 1
                    if piece[1]:
                        sp.append((b.at + 0.5, "out", piece[2]))
                if on_pe:
                    break
        jobs = [j for j in jobs if j[1]]
        now += max((TILE if b.tile else 0) + MM * len(b.steps) + pe_side, STEP * len(b.steps),
                   (1.1 if b.tile else 0) + dve_side, 0.3)
        while asked_gather < len(gathers):
            c, bl = gathers[asked_gather]
            last = beat_of_tile.get(c.g0 + c.S - 1)
            if last is None or b.at < last + 2 or asked_gather >= next_add + 4:
                break
            if c.second and next_route == c.index + 1 < len(chunks) and t >= (chunks[next_route].blk + chunks[next_route].nblk) * BLK:
                break
            start = max(pool_free, now + LATENCY)
            pool_free = start + (c.J // c.nblk) * ROW
            back_at[asked_gather] = pool_free + LATENCY
            requests.append(("gather", c, bl, asked_gather))
            asked_gather += 1
        for n in list(back_at):
            if now >= back_at[n]:
                del back_at[n]
                c, bl = gathers[n]
                blk = c.blk + bl
                jobs.append([9 if c.second else blk / 10, [("add", c.second, blk)] + ([] if c.second else recurrence(blk)), b.at + 1])
        for c in chunks:
            for blk in range(c.blk, c.blk + c.nblk):
                if c.second and t >= (blk + 1) * BLK and blk not in hadd_asked:
                    hadd_asked.add(blk)
                    last = blk == c.blk + c.nblk - 1
                    first = [("hadd", blk, 0)] + [("stats", c, (blk - c.blk) * TURN // PIECE + i) for i in range(TURN // PIECE)]
                    jobs.append([8 + c.index, first + (routing(c)[c.J // PIECE:] if last else []), b.at + 1])
        beats.append(b)
    return beats, requests, sp, beat_of_tile, ready_beat


def build(nc, x, Wi, bi, Wh, bh, router_w, expert_fc, expert_proj, out):
    B, T, D = x.shape
    E, _, HD = expert_fc.shape
    HC = HD // P
    TH = P // B
    NBLK = T // BLK
    JB = BLK // TH
    NT = NBLK * JB
    ZS = 512 // B

    chunks = plan_chunks(JB, E)
    JMAX = max(c.J for c in chunks)
    TMAX = JMAX + E
    beats, pool_dmas, outs, beat_of_tile, ready_beat = plan_beats(chunks, NBLK, T, ZS)
    block_number = {(c.second, c.blk + i): c.b0 + i for c in chunks for i in range(c.nblk)}
    pair_end = [c.g0 + min(2 * q + 2, c.S) for c in chunks for q in range(c.NP)]
    tile_at = lambda n: beats[n].tile if 0 <= n < len(beats) else None

    with ExitStack() as ctx:
        def sb(name, shape, dt=F32):
            return ctx.enter_context(nc.sbuf_tensor(name, shape, dt))

        def psum(name):
            return ctx.enter_context(nc.psum_tensor(name, [P, 512], F32))

        def sem(name):
            return ctx.enter_context(nc.semaphore(name))

        xs_dram = [nc.dram_tensor(f"xs_dram{i}", [TMAX * P, D], F32).ap() for i in range(REGIONS)]
        ys_dram = [nc.dram_tensor(f"ys_dram{i}", [TMAX * P, D], F32).ap() for i in range(REGIONS)]

        x_sb = sb("x_sb", [P, NT, D])
        xnf = sb("xnf", [P, XNF, D])
        xns = sb("xns", [P, JB, D])
        back = sb("back", [P, 4, JB, D])
        xnT = sb("xnT", [P, 4, JB, P])
        hsT = sb("hsT", [P, (T + 1) * B])
        fc_sb = sb("fc_sb", [P, E * HD])
        projT = sb("projT", [P, E * HC * D])
        proj_raw = back[:, :, :, :].rearrange("p a b c -> p (a b c)")[:, 0:E * HD].rearrange("p (e h) -> p e h", e=E)
        w_raw = sb("w_raw", [P, 2, D])
        rw_raw = sb("rw_raw", [E, D])
        wT = sb("wT", [P, 2 * P + E])
        WiT, WhT, rwT = wT[:, 0:P], wT[:, P:2 * P], wT[:, 2 * P:2 * P + E]
        bias2 = sb("bias2", [P, 2])
        bias = sb("bias", [P, 1])
        ident = sb("ident", [P, P])
        before = sb("before", [P, P], BF16)
        ones = sb("ones", [P, P], BF16)
        zeros = sb("zeros", [P, 512])
        kio_i = sb("kio_i", [P, 64], I32)
        kio = sb("kio", [P, 64])
        thr = sb("thr", [P, JMAX])
        pref = sb("pref", [P, E])
        lower = sb("lower", [P, E, E])
        warm = sb("warm", [P, 1])
        stats = sb("stats", [P, 3, JMAX, 6])
        mv = sb("mv", [P, 3, JMAX, 2])
        rstd = sb("rstd", [P, 3, JMAX])
        var_eps = sb("var_eps", [P, 3, JMAX])
        newton = sb("newton", [P, JMAX])
        root_bits = sb("root_bits", [P, JMAX], I32)
        xrt = sb("xrt", [P, 2, 512])
        best = sb("best", [P, JMAX])
        eq = sb("eq", [P, JMAX, E])
        wgt = sb("wgt", [P, JMAX, E])
        oh = sb("oh", [P, JMAX, E], BF16)
        cmp = sb("cmp", [P, E, JMAX])
        ntile = sb("ntile", [P, E])
        tmp8 = sb("tmp8", [P, E, E])
        first_tile = sb("first_tile", [P, E])
        end_tile = sb("end_tile", [P, E])
        posw = sb("posw", [P, JMAX, E])
        posf = sb("posf", [P, JMAX])
        pos = sb("pos", [P, len(chunks), JMAX], I32)
        cmp2 = sb("cmp2", [P, TMAX, E])
        exf = sb("exf", [P, TMAX])
        eoff = sb("eoff", [P, len(chunks), TMAX], I32)
        xs_sb = sb("xs_sb", [P, 6, D])
        xT_sb = sb("xT_sb", [P, 2, P])
        w_sb = sb("w_sb", [P, 2, HD])
        r_sb = sb("r_sb", [P, 2, HD])
        s_sb = sb("s_sb", [P, 2, HC, P])
        y_sb = sb("y_sb", [P, 4, D])

        z = ctx.enter_context(nc.psum_tensor("z", [P, 2, 512], F32))
        mT = psum("mT")
        hp = ctx.enter_context(nc.psum_tensor("hp", [P, 2, 512], F32))
        xTp, yp, lg = psum("xTp"), psum("yp"), psum("lg")

        s_in = [sem(f"s_in{i}") for i in range(NBLK)]
        s_w = sem("s_w")
        s_fc = sem("s_fc")
        s_pr = sem("s_pr")
        s_const = sem("s_const")
        s_kc = sem("s_kc")
        s_zero = [sem(f"s_zero{i}") for i in range(REGIONS)]
        s_dve = sem("s_dve")
        s_tr = sem("s_tr")
        s_evac = sem("s_evac")
        s_xnf = sem("s_xnf")
        s_xns = sem("s_xns")
        s_rt = sem("s_rt")
        s_oh = sem("s_oh")
        s_rank = sem("s_rank")
        s_pos = sem("s_pos")
        s_eoff = sem("s_eoff")
        s_scat = [sem(f"s_scat{i}") for i in range(len(chunks))]
        s_gath = [sem(f"s_gath{i}") for i in range(2 * NBLK)]
        s_add = sem("s_add")
        s_load = sem("s_load")
        s_t0 = sem("s_t0")
        s_xt = sem("s_xt")
        s_m1 = sem("s_m1")
        s_wst = sem("s_wst")
        s_relu = sem("s_relu")
        s_sq = sem("s_sq")
        s_m2 = sem("s_m2")
        s_y = sem("s_y")
        s_store = sem("s_store")
        s_xi = sem("s_xi")
        s_z = sem("s_z")
        s_mm = sem("s_mm")
        s_h = sem("s_h")
        s_out = sem("s_out")

        block = ctx.enter_context(nc.Block())

        def tokens(dram, blk):
            return dram[:, blk * BLK:(blk + 1) * BLK, :].rearrange("b (th j) d -> th b (j d)", th=TH)

        def sb_block(blk):
            return x_sb[:, blk * JB:(blk + 1) * JB, :].rearrange("p j d -> p (j d)")

        def state(t):
            blk, r = divmod(t, BLK)
            th, j = divmod(r, JB)
            at = B + blk * BLK * B + j * P + th * B
            return hsT[:, at:at + B]

        def z_step(t):
            zc, s = divmod(t, ZS)
            return z[:, zc % 2, s * B:(s + 1) * B]

        def pair(c, k):
            return c.q0 + k // 2

        def x_buf(c, k):
            return pair(c, k) % 3 * 2 + k % 2

        def y_buf(c, k):
            return pair(c, k) % 2 * 2 + k % 2

        @block.sync
        def _(sp):
            sp.dma_start(sb_block(0), tokens(x, 0)).then_inc(s_in[0], 16)
            sp.dma_start(rw_raw[:, :], router_w).then_inc(s_w, 16)
            sp.dma_start(w_raw[:, 0, :], Wi).then_inc(s_w, 16)
            sp.dma_start(w_raw[:, 1, :], Wh).then_inc(s_w, 16)
            sp.dma_start(bias2[:, 0:1], bi.rearrange("(p a) -> p a", a=1)).then_inc(s_w, 16)
            sp.dma_start(bias2[:, 1:2], bh.rearrange("(p a) -> p a", a=1)).then_inc(s_w, 16)
            sp.dma_start(fc_sb[:, :].rearrange("p (e h) -> p e h", e=E),
                         expert_fc.rearrange("e d h -> d e h")).then_inc(s_fc, 16)
            sp.wait_ge(s_const, 1)

            def zero(i):
                sp.dma_start(xs_dram[i].rearrange("(p r c) d -> p r (c d)", p=P, c=4),
                             zeros[:, :].unsqueeze(1).to_broadcast([P, TMAX // 4, 512])).then_inc(s_zero[i], 16)

            zero(0)
            sp.dma_start(sb_block(1), tokens(x, 1)).then_inc(s_in[1], 16)
            sp.dma_start(proj_raw, expert_proj.rearrange("e d h -> d e h")).then_inc(s_pr, 16)
            zero(1)
            for blk in range(2, 4):
                sp.dma_start(sb_block(blk), tokens(x, blk)).then_inc(s_in[blk], 16)

            def load(c, q):
                Q = c.q0 + q
                sp.wait_ge(s_scat[c.index], 16 * c.J)
                if Q:
                    sp.wait_ge(s_load, 16 * Q)
                if Q >= 3:
                    sp.wait_ge(s_t0, pair_end[Q - 3])
                sp.dma_start(xs_sb[:, Q % 3 * 2:Q % 3 * 2 + 2, :],
                             xs_dram[c.region][2 * q * P:2 * (q + 1) * P, :].rearrange("(a p) d -> p a d", p=P)
                             ).then_inc(s_load, 16)

            def store(c, q):
                Q, n = c.q0 + q, min(2, c.S - 2 * q)
                sp.wait_ge(s_y, pair_end[Q])
                if Q:
                    sp.wait_ge(s_store, 16 * Q)
                if q == 0 and c.index >= REGIONS:
                    d = chunks[c.index - REGIONS]
                    for m in range(d.b0, d.b0 + d.nblk):
                        sp.wait_ge(s_gath[m], 16 * JB)
                sp.dma_start(ys_dram[c.region][2 * q * P:(2 * q + n) * P, :].rearrange("(a p) d -> p a d", p=P),
                             y_sb[:, Q % 2 * 2:Q % 2 * 2 + n, :]).then_inc(s_store, 16)

            dmas = [(at, "out", blk, None) for at, _, blk in outs]
            dmas += [(beat_of_tile[0] + 0.1 * i, "zero", i, None) for i in range(2, REGIONS)]
            dmas += [(beat_of_tile[0] + 0.5 + IN_BEATS * (blk - 4), "in", blk, None) for blk in range(4, NBLK)]
            for c in chunks:
                for q in range(c.NP):
                    Q = c.q0 + q
                    start = beat_of_tile[c.g0] - 3.2
                    if Q >= 3:
                        start = max(start, beat_of_tile[pair_end[Q - 3] - 1] - 0.9)
                    dmas.append((start, "load", c, q))
                    dmas.append((beat_of_tile[pair_end[Q] - 1] + 1.8, "store", c, q))
            for at, what, c, q in sorted(dmas, key=lambda d: d[0]):
                if what == "load":
                    load(c, q)
                elif what == "store":
                    store(c, q)
                elif what == "zero":
                    zero(c)
                elif what == "in":
                    sp.dma_start(sb_block(c), tokens(x, c)).then_inc(s_in[c], 16)
                else:
                    sp.wait_ge(s_add, block_number[True, c] + 1)
                    sp.dma_start(tokens(out, c), sb_block(c)).then_inc(s_out, 16)
            for zeroed in s_zero:
                sp.wait_ge(zeroed, 16)
            sp.wait_ge(s_store, 16 * (chunks[-1].q0 + chunks[-1].NP))
            sp.wait_ge(s_out, 16 * NBLK)

        @block.gpsimd
        def _(pool):
            pool.memset(zeros[:, :], 0.0).then_inc(s_const, 1)
            pool.memset(hsT[:, 0:B], 0.0).then_inc(s_const, 1)
            pool.memset(ident[:, :], 0.0).then_inc(s_const, 1)
            pool.memset(before[:, :], 1.0).then_inc(s_const, 1)
            pool.memset(ones[:, :], 1.0).then_inc(s_const, 1)
            pool.iota(kio_i[:, :], pattern=[[1, 64]], base=0, channel_multiplier=0).then_inc(s_const, 1)
            pool.wait_ge(s_const, 6)
            pool.affine_select(out=ident[:, :], in_=ident[:, :], compare_op=ALU.not_equal, fill=1.0, base=0,
                               pattern=[[-1, P]], channel_multiplier=1).then_inc(s_const, 1)
            pool.affine_select(out=before[:, :], in_=before[:, :], compare_op=ALU.is_gt, fill=0.0, base=0,
                               pattern=[[1, P]], channel_multiplier=-1).then_inc(s_const, 1)

            def scatter(c):
                pool.wait_ge(s_pos, c.index + 1)
                pool.wait_ge(s_xnf, c.m0 + c.J)
                if c.index < REGIONS:
                    pool.wait_ge(s_zero[c.index], 16)
                else:
                    d = chunks[c.index - REGIONS]
                    pool.wait_ge(s_load, 16 * (d.q0 + d.NP))
                for j in range(c.J):
                    pool.indirect_dma_start(
                        out=xs_dram[c.region], in_=xnf[:, c.x0 + j, :], in_offset=None,
                        out_offset=bass.IndirectOffsetOnAxis(ap=pos[:, c.index, j:j + 1].bitcast(U32), axis=0),
                    ).then_inc(s_scat[c.index], 16)

            def gather(c, bl, n):
                pool.wait_ge(s_store, 16 * (c.q0 + c.NP))
                if n >= 4:
                    pool.wait_ge(s_add, n - 3)
                for j in range(JB):
                    pool.indirect_dma_start(
                        out=back[:, n % 4, j, :], out_offset=None, in_=ys_dram[c.region][0:c.S * P, :],
                        in_offset=bass.IndirectOffsetOnAxis(ap=pos[:, c.index, bl * JB + j:bl * JB + j + 1].bitcast(U32), axis=0)
                    ).then_inc(s_gath[n], 16)

            for what in pool_dmas:
                if what[0] == "scatter":
                    scatter(what[1])
                else:
                    gather(*what[1:])

        @block.vector
        def _(dve):
            count = {"chain": 0, "groups": 0}
            hadd_groups = {}

            def link(ins):
                count["chain"] += 1
                ins.then_inc(s_dve, 1)
                dve.wait_ge(s_dve, count["chain"])

            def evacuate(out_ap, n=512):
                count["groups"] += 1
                dve.wait_ge(s_tr, count["groups"])
                dve.tensor_copy(out_ap, mT[:, 0:n]).then_inc(s_evac, 1)

            def statistics(w, n0, tiles):
                for j in tiles:
                    dve.bn_stats(stats[:, w, j, :], x_sb[:, n0 + j, :]).then_inc(s_dve, 1)
                count["chain"] += len(tiles)
                dve.wait_ge(s_dve, count["chain"])
                for j in tiles:
                    dve.bn_aggr(mv[:, w, j, :], stats[:, w, j, :]).then_inc(s_dve, 1)
                count["chain"] += len(tiles)

            def inverse_root(w, J, part):
                v, y, t, r = var_eps[:, w, 0:J], rstd[:, w, 0:J], newton[:, 0:J], root_bits[:, 0:J]
                if part == 0:
                    dve.wait_ge(s_dve, count["chain"])
                    link(dve.tensor_scalar(v, mv[:, w, 0:J, 1], EPS, None, ALU.add))
                    link(dve.tensor_scalar(r, v.bitcast(I32), 1, None, ALU.arith_shift_right))
                    link(dve.tensor_scalar(y.bitcast(I32), r, -1.0, float(0x5F3759DF), ALU.mult, ALU.add))
                for _ in range(1 + part):
                    link(dve.tensor_tensor(t, y, y, ALU.mult))
                    link(dve.scalar_tensor_tensor(out=t, in0=t, scalar=-0.5, in1=v, op0=ALU.mult, op1=ALU.mult))
                    link(dve.scalar_tensor_tensor(out=y, in0=t, scalar=1.5, in1=y, op0=ALU.add, op1=ALU.mult))

            def normalise(w, n0, tiles, dst, x0, done):
                for j in tiles:
                    dve.tensor_scalar(dst[:, x0 + j, :], x_sb[:, n0 + j, :], mv[:, w, j, 0:1], rstd[:, w, j:j + 1],
                                      ALU.subtract, ALU.mult).then_inc(done, 1)

            def pick(c):
                J = c.J
                lg3 = lg[:, 0:J * E].rearrange("p (j e) -> p j e", e=E)
                dve.wait_ge(s_rt, (c.m0 + J) // 4)
                link(dve.tensor_reduce(best[:, 0:J], lg3, AX_X, ALU.max))
                link(dve.tensor_tensor(eq[:, 0:J, :], lg3, best[:, 0:J].unsqueeze(2).to_broadcast([P, J, E]), ALU.is_ge))
                link(dve.tensor_tensor(wgt[:, 0:J, :], eq[:, 0:J, :], pref[:, :].unsqueeze(1).to_broadcast([P, J, E]), ALU.mult))
                link(dve.tensor_reduce(best[:, 0:J], wgt[:, 0:J, :], AX_X, ALU.max))
                dve.tensor_tensor(oh[:, 0:J, :], wgt[:, 0:J, :], best[:, 0:J].unsqueeze(2).to_broadcast([P, J, E]),
                                  ALU.is_equal).then_inc(s_oh, 1)

            def slots(c):
                J, S = c.J, c.S
                rk3 = lg[:, 0:(J + 1) * E].rearrange("p (j e) -> p j e", e=E)
                dve.wait_ge(s_rank, c.index + 1)
                link(dve.tensor_tensor(cmp[:, :, 0:J], rk3[:, J, :].unsqueeze(2).to_broadcast([P, E, J]),
                                       thr[:, 0:J].unsqueeze(1).to_broadcast([P, E, J]), ALU.is_gt))
                link(dve.tensor_reduce(ntile[:, :], cmp[:, :, 0:J], AX_X, ALU.add))
                link(dve.tensor_tensor(tmp8[:, :, :], lower[:, :, :], ntile[:, :].unsqueeze(1).to_broadcast([P, E, E]), ALU.mult))
                link(dve.tensor_reduce(first_tile[:, :], tmp8[:, :, :], AX_X, ALU.add))
                dve.tensor_tensor(end_tile[:, :], first_tile[:, :], ntile[:, :], ALU.add).then_inc(s_dve, 1)
                count["chain"] += 1
                link(dve.scalar_tensor_tensor(out=posw[:, 0:J, :], in0=first_tile[:, :].unsqueeze(1).to_broadcast([P, J, E]),
                                              scalar=float(P), in1=rk3[:, 0:J, :], op0=ALU.mult, op1=ALU.add))
                link(dve.tensor_tensor(posw[:, 0:J, :], posw[:, 0:J, :], oh[:, 0:J, :], ALU.mult))
                link(dve.tensor_reduce(posf[:, 0:J], posw[:, 0:J, :], AX_X, ALU.add))
                dve.tensor_scalar(pos[:, c.index, 0:J], posf[:, 0:J], float(S * P - 1), None, ALU.min).then_inc(s_pos, 1)

            def experts(c):
                S = c.S
                link(dve.tensor_tensor(cmp2[:, 0:S, :], kio[:, 0:S].unsqueeze(2).to_broadcast([P, S, E]),
                                       end_tile[:, :].unsqueeze(1).to_broadcast([P, S, E]), ALU.is_ge))
                link(dve.tensor_reduce(exf[:, 0:S], cmp2[:, 0:S, :], AX_X, ALU.add))
                dve.tensor_scalar(eoff[:, c.index, 0:S], exf[:, 0:S], float(E - 1), float(HD), ALU.min, ALU.mult
                                  ).then_inc(s_eoff, 1)

            def copy_xT(c, k):
                g = c.g0 + k
                dve.wait_ge(s_t0, g + 1)
                if g >= 2:
                    dve.wait_ge(s_m1, g - 1)
                dve.tensor_copy(xT_sb[:, g % 2, :], xTp[:, 0:P]).then_inc(s_xt, 1)

            def relu(c, k):
                g = c.g0 + k
                dve.wait_ge(s_m1, g + 1)
                if g >= 2:
                    dve.wait_ge(s_sq, 2 * (g - 1))
                dve.tensor_scalar(r_sb[:, g % 2, :], hp[:, g % 2, :], 0.0, None, ALU.max).then_inc(s_relu, 1)

            def halve(c, k):
                dve.wait_ge(s_m2, c.g0 + k + 1)
                if pair(c, k) >= 2 and k % 2 == 0:
                    dve.wait_ge(s_store, 16 * (pair(c, k) - 1))
                dve.tensor_scalar(y_sb[:, y_buf(c, k), :], yp[:, 0:D], 0.5, None, ALU.mult).then_inc(s_y, 1)

            def turned(what, c, i, g):
                n = 2 * i + g
                if what == "turn":
                    if c.m0 // 4 + n >= 2:
                        dve.wait_ge(s_rt, c.m0 // 4 + n - 1)
                    evacuate(xrt[:, n % 2, :])
                elif what == "turn2":
                    if c >= 4 and n == 0:
                        dve.wait_ge(s_xi, (c - 3) * (BLK // ZS))
                    evacuate(xnT[:, c % 4, 4 * n:4 * n + 4, :].rearrange("p j t -> p (j t)"))
                elif what == "hadd":
                    v = x_sb[:, c * JB + 4 * n:c * JB + 4 * n + 4, :].rearrange("p j d -> p (j d)")
                    count["groups"] += 1
                    dve.wait_ge(s_tr, count["groups"])
                    dve.tensor_tensor(v, v, mT[:, :], ALU.add).then_inc(s_evac, 1)
                    hadd_groups[c] = count["groups"]
                else:
                    evacuate(projT[:, n * 512:(n + 1) * 512])

            def other(what, c, i):
                if what == "stats":
                    if c.second:
                        dve.wait_ge(s_evac, hadd_groups[c.blk + PIECE * i // JB])
                    else:
                        dve.wait_ge(s_in[c.blk + PIECE * i // JB], 16)
                    statistics(c.index % 2, c.n0, range(PIECE * i, PIECE * (i + 1)))
                elif what == "root":
                    inverse_root(c.index % 2, c.J, i)
                elif what == "norm":
                    if i == 0:
                        for d in chunks[max(c.index - 4, 0):c.index]:
                            if d.x0 < c.x0 + c.J and c.x0 < d.x0 + d.J:
                                dve.wait_ge(s_scat[d.index], 16 * d.J)
                    normalise(c.index % 2, c.n0, range(PIECE * i, PIECE * (i + 1)), xnf, c.x0, s_xnf)
                elif what == "pick":
                    pick(c)
                elif what == "slots":
                    slots(c)
                elif what == "experts":
                    experts(c)
                elif what == "add":
                    n = block_number[c, i]
                    dve.wait_ge(s_gath[n], 16 * JB)
                    v = sb_block(i)
                    dve.tensor_tensor(v, v, back[:, n % 4, :, :].rearrange("p j d -> p (j d)"), ALU.add).then_inc(s_add, 1)
                elif what == "stats2":
                    dve.wait_ge(s_add, block_number[False, c] + 1)
                    statistics(2, c * JB, range(PIECE * i, PIECE * (i + 1)))
                elif what == "root2":
                    inverse_root(2, JB, i)
                elif what == "norm2":
                    normalise(2, c * JB, range(PIECE * i, PIECE * (i + 1)), xns, 0, s_xns)
                elif what == "bias":
                    dve.wait_ge(s_xi, i + 1)
                    zb = z[:, i % 2, :]
                    dve.tensor_scalar(zb, zb, bias[:, 0:1], None, ALU.add).then_inc(s_z, 1)

            dve.wait_ge(s_const, 8)
            link(dve.tensor_copy(kio[:, :], kio_i[:, :]))
            dve.tensor_scalar(thr[:, :], kio[:, 0:JMAX], float(P), None, ALU.mult).then_inc(s_kc, 1)
            dve.tensor_scalar(pref[:, :], kio[:, 0:E], -1.0, float(E), ALU.mult, ALU.add).then_inc(s_kc, 1)
            dve.tensor_tensor(lower[:, :, :], kio[:, 0:E].unsqueeze(1).to_broadcast([P, E, E]),
                              kio[:, 0:E].unsqueeze(2).to_broadcast([P, E, E]), ALU.is_lt).then_inc(s_kc, 1)
            dve.wait_ge(s_w, 80)
            dve.tensor_tensor(bias[:, :], bias2[:, 0:1], bias2[:, 1:2], ALU.add).then_inc(s_kc, 1)
            dve.wait_ge(s_kc, 4)
            evacuate(wT[:, :], 2 * P + E)

            for b in beats:
                now, after, last = b.tile, tile_at(b.at + 1), tile_at(b.at - 1)
                turning = [p for p in b.side if p[0] in TURNING]
                if after:
                    copy_xT(*after)
                if b.steps:
                    for p in turning:
                        turned(*p, 0)
                if now:
                    relu(*now)
                if b.steps:
                    for p in turning:
                        turned(*p, 1)
                if last:
                    halve(*last)
                if not b.steps:
                    for p in turning:
                        turned(*p, 0)
                        turned(*p, 1)
                for p in b.side:
                    if p[0] not in TURNING:
                        other(*(p + (None,))[:3])

        @block.scalar
        def _(act):
            act.wait_ge(s_const, 1)
            act.activation(warm[:, :], zeros[:, 0:1], ACT.Tanh)

            def tanh(t):
                act.wait_ge(s_mm, t + 1)
                act.activation(state(t), z_step(t), ACT.Tanh).then_inc(s_h, 1)

            offsets = {}

            def load_offset(c, k):
                if k == 0:
                    act.wait_ge(s_eoff, c.index + 1)
                offsets[c.g0 + k] = nc.values_load(eoff[0:1, c.index, k:k + 1], engines=[mybir.EngineType.Activation], min_val=0,
                                                   max_val=(E - 1) * HD, skip_runtime_bounds_check_because="clamped where it is computed")

            def stage(c, k, half):
                g, w = c.g0 + k, HD // 2
                if half == 0:
                    if g == 0:
                        act.wait_ge(s_fc, 16)
                    if g >= 2:
                        act.wait_ge(s_m1, g - 1)
                act.activation(w_sb[:, g % 2, half * w:(half + 1) * w], fc_sb[:, bass.ds(offsets[g] + half * w, w)],
                               ACT.Copy).then_inc(s_wst, 1)

            def square(c, k, half):
                g, w = c.g0 + k, HC // 2
                if half == 0:
                    act.wait_ge(s_relu, g + 1)
                    if g >= 2:
                        act.wait_ge(s_m2, g - 1)
                act.activation(s_sb[:, g % 2, half * w:(half + 1) * w, :].rearrange("p c t -> p (c t)"),
                               r_sb[:, g % 2, half * w * P:(half + 1) * w * P], ACT.Square).then_inc(s_sq, 1)

            for b in beats:
                after, last = tile_at(b.at + 1), tile_at(b.at - 1)
                for i in range(BEAT):
                    if i < len(b.steps):
                        tanh(b.steps[i])
                    if last and i < 2:
                        square(*last, i)
                    if after and i == 1:
                        load_offset(*after)
                    if after and i >= 2:
                        stage(*after, i - 2)

        @block.tensor
        def _(pe):
            groups = [0]
            offsets = {}

            def transpose4(ins):
                if groups[0]:
                    pe.wait_ge(s_evac, groups[0])
                groups[0] += 1
                at = 0
                for a in ins:
                    rows = a.shape[0]
                    last = pe.transpose(mT[:, at:at + rows], a, ident[0:rows, 0:rows])
                    at += rows
                last.then_inc(s_tr, 1)

            def logits(c, n):
                if n == 0 and c.index:
                    pe.wait_ge(s_eoff, c.index)
                pe.wait_ge(s_evac, turn_at[n])
                for q in range(4):
                    j = 4 * n + q
                    mm = pe.matmul(lg[:, j * E:(j + 1) * E], xrt[:, n % 2, q * P:(q + 1) * P], rwT, start=True, stop=True)
                mm.then_inc(s_rt, 1)

            turn_at, xnT_at = {}, {}

            def turn(what, c, i, g):
                n = 2 * i + g
                if what == "turn":
                    if i:
                        logits(c, n - 2)
                    pe.wait_ge(s_xnf, c.m0 + 4 * n + 4)
                    transpose4([xnf[:, c.x0 + 4 * n + q, :] for q in range(4)])
                    turn_at[n] = groups[0]
                elif what == "turn2":
                    pe.wait_ge(s_xns, c * JB + 4 * n + 4)
                    transpose4([xns[:, 4 * n + q, :] for q in range(4)])
                    xnT_at[c] = groups[0]
                elif what == "hadd":
                    pe.wait_ge(s_h, (c + 1) * BLK)
                    at = B + c * BLK * B + 4 * n * P
                    transpose4([hsT[:, at + q * P:at + (q + 1) * P] for q in range(4)])
                else:
                    pe.wait_ge(s_pr, 16)
                    transpose4([proj_raw[:, n, h * P:(h + 1) * P] for h in range(HC)])

            def rank(c):
                pe.wait_ge(s_oh, c.index + 1)
                n = c.J * E
                ohc = oh[:, 0:c.J, :].rearrange("p j e -> p (j e)")
                pe.matmul(lg[:, 0:n], before[:, :], ohc, start=True, stop=False, skip_group_check=True)
                for s in range(1, c.J + 1):
                    mm = pe.matmul(lg[:, s * E:n + E], ones[:, :], ohc[:, 0:n + E - s * E], start=False,
                                   stop=(s == c.J), skip_group_check=True)
                mm.then_inc(s_rank, 1)

            def load_offset(c, k):
                if k == 0:
                    pe.wait_ge(s_eoff, c.index + 1)
                offsets[c.g0 + k] = nc.values_load(eoff[0:1, c.index, k:k + 1], engines=[mybir.EngineType.PE], min_val=0,
                                                   max_val=(E - 1) * HD, skip_runtime_bounds_check_because="clamped where it is computed")

            def turn_x(c, k):
                g = c.g0 + k
                pe.wait_ge(s_load, 16 * (pair(c, k) + 1))
                if g:
                    pe.wait_ge(s_xt, g)
                pe.transpose(xTp[:, 0:P], xs_sb[:, x_buf(c, k), :], ident[:, :]).then_inc(s_t0, 1)

            def product1(c, k, half):
                g = c.g0 + k
                if half == 0:
                    pe.wait_ge(s_xt, g + 1)
                    if g >= 2:
                        pe.wait_ge(s_relu, g - 1)
                pe.wait_ge(s_wst, 2 * g + 1 + half)
                for h in range(half * HC // 2, (half + 1) * HC // 2):
                    mm = pe.matmul(hp[:, g % 2, h * P:(h + 1) * P], w_sb[:, g % 2, h * P:(h + 1) * P], xT_sb[:, g % 2, :],
                                   start=True, stop=True)
                if half:
                    mm.then_inc(s_m1, 1)

            def product2(c, k, h):
                g = c.g0 + k
                if h % 2 == 0:
                    pe.wait_ge(s_sq, 2 * g + 1 + h // 2)
                if h == 0 and g:
                    pe.wait_ge(s_y, g)
                mm = pe.matmul(yp[:, 0:D], s_sb[:, g % 2, h, :], projT[:, bass.ds(offsets[g] + h * D, D)],
                               start=(h == 0), stop=(h == HC - 1))
                if h == HC - 1:
                    mm.then_inc(s_m2, 1)

            def inputs(zc, q):
                blk, w = divmod(zc, BLK // ZS)
                if q == 0:
                    pe.wait_ge(s_evac, xnT_at[blk])
                th = w * (ZS // JB) + q
                mm = pe.matmul(z[:, zc % 2, q * P:(q + 1) * P], WiT, xnT[:, blk % 4, :, th * B:(th + 1) * B],
                               start=(q == 0), stop=False, skip_group_check=True)
                if q == 3:
                    mm.then_inc(s_xi, 1)

            def step(t):
                zc, s = divmod(t, ZS)
                if s == 0:
                    pe.wait_ge(s_z, zc + 1)
                if t:
                    pe.wait_ge(s_h, t)
                pe.matmul(z_step(t), WhT, state(t - 1), start=False, stop=True, skip_group_check=True).then_inc(s_mm, 1)
                if 4 <= s < 8 and zc + 1 < T // ZS:
                    inputs(zc + 1, s - 4)

            pe.wait_ge(s_const, 8)
            pe.wait_ge(s_w, 80)
            transpose4([w_raw[:, 0, :], w_raw[:, 1, :], rw_raw[:, :]])
            pe.wait_ge(s_evac, 1)

            for b in beats:
                now, after, last = b.tile, tile_at(b.at + 1), tile_at(b.at - 1)
                turning = [p for p in b.side if p[0] in TURNING]
                if len(b.steps) > 0:
                    step(b.steps[0])
                if after:
                    turn_x(*after)
                if now:
                    product1(*now, 0)
                if b.steps:
                    for p in turning:
                        turn(*p, 0)
                if len(b.steps) > 1:
                    step(b.steps[1])
                if now:
                    product1(*now, 1)
                if b.steps:
                    for p in turning:
                        turn(*p, 1)
                if len(b.steps) > 2:
                    step(b.steps[2])
                if last:
                    product2(*last, 0)
                    product2(*last, 1)
                if len(b.steps) > 3:
                    step(b.steps[3])
                if last:
                    product2(*last, 2)
                    product2(*last, 3)
                if after:
                    load_offset(*after)
                if not b.steps:
                    for p in turning:
                        turn(*p, 0)
                        turn(*p, 1)
                for p in b.side:
                    if p[0] == "logits":
                        logits(p[1], p[1].J // 4 - 2)
                        logits(p[1], p[1].J // 4 - 1)
                    elif p[0] == "rank":
                        rank(p[1])
                    elif p[0] == "xi0":
                        for q in range(4):
                            inputs(0, q)


_INS = ['L0_attn_x', 'L0_attn_Wi', 'L0_attn_bi', 'L0_attn_Wh', 'L0_attn_bh', 'L0_ffn_router_w', 'L0_ffn_expert_fc',
        'L0_ffn_expert_proj']
_OUTS = [((16, 512, 128), 'float32')]


def kernel(**inputs):
    import numpy as _np
    import concourse.bacc as _bacc
    from concourse import mybir as _mybir
    from concourse.bass_utils import run_bass_kernel_spmd as _run

    nc = _bacc.Bacc("TRN2", target_bir_lowering=False, num_devices=1)
    arrays, args = {}, []
    for name in _INS:
        a = _np.ascontiguousarray(inputs[name])
        arrays[f"in_{name}_dram"] = a
        args.append(nc.dram_tensor(f"in_{name}_dram", a.shape, _mybir.dt.from_np(a.dtype), kind="ExternalInput").ap())
    for i, (shape, dtype) in enumerate(_OUTS):
        dt = _mybir.dt.from_np(_np.dtype(dtype))
        args.append(nc.dram_tensor(f"out_{i}_dram", shape, dt, kind="ExternalOutput").ap())
    build(nc, *args)
    r = _run(nc, [arrays], core_ids=[0])
    return r.results[0]["out_0_dram"]
```
